# Optimizing a Trainium2 kernel written in Bass

```python
import numpy as np
import jax
import jax.numpy as jnp

def _softmax(x, axis=-1):
    return jax.nn.softmax(x, axis=axis)

def _gelu(x):
    return jax.nn.gelu(x, approximate=True)

def _silu(x):
    return jax.nn.silu(x)

def _sigmoid(x):
    return jax.nn.sigmoid(x)

def _layernorm(x, axis=-1, eps=1e-05):
    m = jnp.mean(x, axis=axis, keepdims=True)
    v = jnp.var(x, axis=axis, keepdims=True)
    return (x - m) / jnp.sqrt(v + eps)

def _scatter_add(tgt, idx, src, axis=0):
    return tgt.at[idx].add(src)

def _segment_sum(src, seg, n):
    return jax.ops.segment_sum(src, seg, n)
kernel_name = 'mk_flamingo_gated_d1_seqx_r4_50b054'

def setup_inputs(seed: int=0):
    np.random.seed(seed)
    _w = jnp.asarray

    def _rec_inputs():
        import jax
        import jax.numpy as jnp
        _rk = jax.random.key(seed)
        x = 7.22e-05 + 1 * jax.random.normal(jax.random.fold_in(_rk, 1), (4, 512, 512), jnp.float32)
        _lenS = 512 - jax.random.randint(jax.random.fold_in(_rk, 7), (4,), 0, max(1, 512 // 4) + 1, jnp.int32)
        _lenS2 = 512 - jax.random.randint(jax.random.fold_in(_rk, 8), (4,), 0, max(1, 512 // 4) + 1, jnp.int32)
        _ctx_1024P = jax.random.normal(jax.random.fold_in(_rk, 11), (4, 16, 256), jnp.float32)
        _ctx_1024c = jax.random.dirichlet(jax.random.fold_in(_rk, 511), 0.3 * jnp.ones((16,), jnp.float32), (4, 512))
        _ctx_1024t = jnp.einsum('bsk,bkd->bsd', _ctx_1024c, _ctx_1024P)
        _ctx_1024t = _ctx_1024t * jax.lax.rsqrt(jnp.mean(jnp.square(_ctx_1024t)) + 1e-12) * 0.953939
        ctx_1024 = 2.81802e-05 + 1.00001 * (_ctx_1024t + 0.3 * jax.random.normal(jax.random.fold_in(_rk, 611), (4, 512, 256), jnp.float32))
        _g = jax.random.normal(jax.random.fold_in(_rk, 9001), (2, 1), jnp.float32)
        _g = jnp.sign(_g) * jnp.maximum(jnp.abs(_g), 1.0) + (_g == 0) * 1.0
        g_xattn = _g[0]
        g_ffn = _g[1]
        return (x, ctx_1024, g_xattn, g_ffn)
    x, ctx_1024, g_xattn, g_ffn = _rec_inputs()

    def _L0_xattn_setup():
        import jax, jax.numpy as jnp
        import numpy as np
        key = jax.random.key(seed)
        ks = jax.random.split(key, 6)
        B, L, N, C, D = (8, 128, 512, 256, 128)
        return {'teacher_logits': jax.random.normal(ks[0], (B, L, N), dtype=jnp.float32), 'teacher_features': jax.random.normal(ks[1], (B, N, C), dtype=jnp.float32), 'Wq': jax.random.normal(ks[2], (D, C), dtype=jnp.float32) * (1.0 / np.sqrt(C)), 'bq': jnp.zeros((D,), dtype=jnp.float32), 'Wk': jax.random.normal(ks[3], (D, C), dtype=jnp.float32) * (1.0 / np.sqrt(C)), 'bk': jnp.zeros((D,), dtype=jnp.float32)}
    _L0_xattn_all = _L0_xattn_setup()
    _L0_xattn_in = {k: v for k, v in _L0_xattn_all.items() if k in ('Wq', 'bq', 'Wk', 'bk')}
    del _L0_xattn_all

    def _L0_ffn_setup():
        import jax, jax.numpy as jnp
        import numpy as np
        EPS = 1e-07
        CURVATURE = 1.0
        MAX_NORM_RATIO = 0.99
        B, L, N, K = (4, 512, 512, 512)

        def _ternary_init(key, n, k):
            rand = jax.random.normal(key, (n, k), dtype=jnp.float32)
            threshold = 0.5 * jnp.mean(jnp.abs(rand))
            return jnp.where(rand > threshold, 1.0, jnp.where(rand < -threshold, -1.0, 0.0)).astype(jnp.float32)
        key = jax.random.key(seed)
        kx, kw = jax.random.split(key)
        x = jax.random.normal(kx, (B, L, N), dtype=jnp.float32)
        weight = _ternary_init(kw, N, K)
        scale = jnp.full((K,), 1.0 / np.sqrt(N), dtype=jnp.float32)
        return {'x': x, 'weight': weight, 'scale': scale}
    _L0_ffn_all = _L0_ffn_setup()
    _L0_ffn_in = {k: v for k, v in _L0_ffn_all.items() if k in ('weight', 'scale')}
    del _L0_ffn_all
    return {'x': x, 'ctx_1024': ctx_1024, 'g_xattn': g_xattn, 'g_ffn': g_ffn, 'L0_xattn_Wq': _L0_xattn_in['Wq'], 'L0_xattn_bq': _L0_xattn_in['bq'], 'L0_xattn_Wk': _L0_xattn_in['Wk'], 'L0_xattn_bk': _L0_xattn_in['bk'], 'L0_ffn_weight': _L0_ffn_in['weight'], 'L0_ffn_scale': _L0_ffn_in['scale']}

def reference(x, ctx_1024, g_xattn, g_ffn, L0_xattn_Wq, L0_xattn_bq, L0_xattn_Wk, L0_xattn_bk, L0_ffn_weight, L0_ffn_scale):
    import jax
    import jax.numpy as jnp

    def _L0_xattn_ref(teacher_logits, teacher_features, Wq, bq, Wk, bk):
        import jax, jax.numpy as jnp
        import numpy as np
        query = jnp.einsum('bnc,dc->bnd', teacher_features, Wq) + bq
        key = jnp.einsum('bnc,dc->bnd', teacher_features, Wk) + bk
        energy = jnp.einsum('bnd,bmd->bnm', query, key)
        attention = jax.nn.softmax(energy, axis=-1)
        x_m = jnp.einsum('bln,bmn->blm', teacher_logits, attention)
        return x_m

    def _L0_ffn_ref(x, weight, scale):
        import jax, jax.numpy as jnp
        import numpy as np
        EPS = 1e-07
        CURVATURE = 1.0
        MAX_NORM_RATIO = 0.99
        B, L, N, K = (4, 512, 512, 512)

        def _ternary_init(key, n, k):
            rand = jax.random.normal(key, (n, k), dtype=jnp.float32)
            threshold = 0.5 * jnp.mean(jnp.abs(rand))
            return jnp.where(rand > threshold, 1.0, jnp.where(rand < -threshold, -1.0, 0.0)).astype(jnp.float32)
        sqrt_c = jnp.sqrt(jnp.float32(CURVATURE))
        out = jnp.einsum('bln,nk->blk', x, weight) * scale
        v_norm = jnp.maximum(jnp.linalg.norm(out, axis=-1, keepdims=True), EPS)
        scaled_norm = sqrt_c * v_norm
        out = out * (jnp.tanh(scaled_norm) / (scaled_norm + EPS))
        max_norm = MAX_NORM_RATIO / sqrt_c
        o_norm = jnp.maximum(jnp.linalg.norm(out, axis=-1, keepdims=True), EPS)
        out = out * jnp.minimum(max_norm / o_norm, 1.0)
        return out.astype(x.dtype)
    x = x + jnp.tanh(g_xattn[0]) * _L0_xattn_ref(_layernorm(x, axis=-1), ctx_1024, L0_xattn_Wq, L0_xattn_bq, L0_xattn_Wk, L0_xattn_bk)
    x = x + jnp.tanh(g_ffn[0]) * _L0_ffn_ref(_layernorm(x, axis=-1), L0_ffn_weight, L0_ffn_scale)
    return x

_drawn_inputs = setup_inputs


def setup_inputs(seed=0):
    import zlib

    import numpy as np

    out = dict(_drawn_inputs(seed))
    spreads = {'L0_xattn_bq': (0.0, 0.1),
     'L0_xattn_bk': (0.0, 0.1),
     'L0_ffn_scale': (0.04419417306780815, 0.2)}
    factors = {}
    for name, (base, spread) in spreads.items():
        noise = np.random.default_rng([zlib.crc32(name.encode()), seed]).standard_normal(out[name].shape)
        drawn = base * np.exp(spread * noise) if base else spread * noise
        out[name] = jnp.asarray(drawn.astype(out[name].dtype))
    for name, factor in factors.items():
        out[name] = (out[name] * factor).astype(out[name].dtype)
    return out
```

```python
from contextlib import ExitStack

import concourse.bass as bass
from concourse import mybir

F32 = mybir.dt.float32
F32R = mybir.dt.float32r
ALU = mybir.AluOpType
ACT = mybir.ActivationFunctionType
AX_X = mybir.AxisListType.X

LN_EPS = 1e-5
NORM_EPS = 1e-7
MAX_NORM = 0.99

TURNS_PROLOGUE = ["W", "C0", "C1", "X0", "P0", "P1", "P2", "P3"]
TURNS_BODY = ["X1", "C0", "C1", "X2", "Z0", "X3", "Z1", "Z2", "X0", "Z3", "P0", "P1", "P2", "P3"]
TURNS_LAST = ["X1", "X2", "Z0", "X3", "Z1", "Z2", "Z3"]


def gated_block(nc, x, ctx, g_xattn, g_ffn, wq, bq, wk, bk, w, scale, out):
    P = 128
    B, S, N = x.shape
    C = ctx.shape[2]
    D = wq.shape[0]
    T = S // P
    CT = C // P
    assert (T, CT, D, N, S) == (4, 2, P, T * P, T * P)
    LAST = B - 1

    def turn(b, name):
        if b is None:
            k = TURNS_PROLOGUE.index(name)
            return k % 2, k + 1
        names = TURNS_LAST if isinstance(b, int) and b == LAST else TURNS_BODY
        k = names.index(name)
        return k % 2, len(TURNS_PROLOGUE) + len(TURNS_BODY) * b + k + 1

    with ExitStack() as stack:
        def sbuf(name, shape, dt=F32):
            return stack.enter_context(nc.sbuf_tensor(name, shape, dt))

        def psum(name):
            return stack.enter_context(nc.psum_tensor(name, [P, 512], F32))

        def sem(name):
            return stack.enter_context(nc.semaphore(name))

        x_rows = sbuf("x_rows", [P, T, N])
        ctx_rows = sbuf("ctx_rows", [P, T, C])
        wqk_rows = sbuf("wqk_rows", [P, 2 * C])
        w_rows = sbuf("w_rows", [P, T, N])
        scale_all = sbuf("scale_all", [P, N])
        b_q = sbuf("b_q", [P, 1])
        b_k = sbuf("b_k", [P, 1])
        gates = sbuf("gates", [P, 2])
        tanh_gates = sbuf("tanh_gates", [P, 2])
        ident = sbuf("ident", [P, P])
        half = sbuf("half", [P, T])
        minus_half = sbuf("minus_half", [P, T])
        wqk_hi, wqk_lo = (sbuf(f"wqk_{s}", [P, 2 * C], F32R) for s in ("hi", "lo"))
        ct_hi, ct_lo = (sbuf(f"ct_{s}", [P, CT, S], F32R) for s in ("hi", "lo"))
        qk_hi, qk_lo = (sbuf(f"qk_{s}", [P, 2, S], F32R) for s in ("hi", "lo"))
        pt_hi, pt_lo = (sbuf(f"pt_{s}", [P, T, S], F32R) for s in ("hi", "lo"))
        xt_hi, xt_lo = (sbuf(f"xt_{s}", [P, 2, N], F32R) for s in ("hi", "lo"))
        zt_hi, zt_lo = (sbuf(f"zt_{s}", [P, 2, N], F32R) for s in ("hi", "lo"))
        w_hi, w_lo = (sbuf(f"w_{s}", [P, T, N], F32R) for s in ("hi", "lo"))
        probs = sbuf("probs", [P, T, S])
        probs_n = sbuf("probs_n", [P, T, S])
        xn = sbuf("xn", [P, T, N])
        y_rows = sbuf("y_rows", [P, T, N])
        z_rows = sbuf("z_rows", [P, 2, N])
        t_rows = sbuf("t_rows", [P, T, N])
        squares = sbuf("squares", [P, N])
        neg_max, exp_sum, inv_sum = (sbuf(n, [P, T]) for n in ("neg_max", "exp_sum", "inv_sum"))
        x_bn, y_bn = (sbuf(n, [P, T, 6]) for n in ("x_bn", "y_bn"))
        x_mv, y_mv = (sbuf(n, [P, T, 2]) for n in ("x_mv", "y_mv"))
        x_ve, x_rstd, x_nm = (sbuf(n, [P, T]) for n in ("x_ve", "x_rstd", "x_nm"))
        y_ve, y_rstd, y_nm = (sbuf(n, [P, T]) for n in ("y_ve", "y_rstd", "y_nm"))
        sq_sum, norm, v_norm, v_eps, v_inv, v_tanh, f_exp, o_raw, o_norm, o_inv, clip, f_all = (
            sbuf(n, [P, T]) for n in ("sq_sum", "norm", "v_norm", "v_eps", "v_inv", "v_tanh", "f_exp",
                                      "o_raw", "o_norm", "o_inv", "clip", "f_all"))

        turn_ps = [psum(f"turn_ps{i}") for i in range(2)]
        front_ps = [psum(f"front_ps{i}") for i in range(2)]
        pv_ps = [psum(f"pv_ps{i}") for i in range(2)]
        ffn_ps = [psum(f"ffn_ps{i}") for i in range(2)]

        ctx_in, wqk_in, small_in, w_in, scale_in = (sem(n) for n in ("ctx_in", "wqk_in", "small_in", "w_in", "scale_in"))
        x_in = [sem(f"x_in{l}") for l in range(T)]
        stored = [sem(f"stored{l}") for l in range(T)]
        turned, hi_done, lo_done = sem("turned"), sem("hi_done"), sem("lo_done")
        consts_done, ident_done, gates_done = sem("consts_done"), sem("ident_done"), sem("gates_done")
        w_hi_done, w_lo_done = sem("w_hi_done"), sem("w_lo_done")
        qk_done, qk_hi_done, qk_lo_done = sem("qk_done"), sem("qk_hi_done"), sem("qk_lo_done")
        energy_done, max_done, exp_done, inv_done, probs_done = (
            sem(n) for n in ("energy_done", "max_done", "exp_done", "inv_done", "probs_done"))
        x_bn_done, x_mv_done, x_ve_done, x_rstd_done, x_nm_done, xn_done = (
            sem(n) for n in ("x_bn_done", "x_mv_done", "x_ve_done", "x_rstd_done", "x_nm_done", "xn_done"))
        pv_done, y_done, y_bn_done, y_mv_done, y_ve_done, y_rstd_done, y_nm_done, z_done = (
            sem(n) for n in ("pv_done", "y_done", "y_bn_done", "y_mv_done", "y_ve_done", "y_rstd_done", "y_nm_done",
                             "z_done"))
        ffn_done, t_done, sq_done, final_done = (sem(n) for n in ("ffn_done", "t_done", "sq_done", "final_done"))
        norm_done, v_norm_done, v_eps_done, v_inv_done, v_tanh_done, f_exp_done, o_raw_done, o_norm_done, o_inv_done, \
            clip_done, gated_done, f_done = (sem(n) for n in ("norm_done", "v_norm_done", "v_eps_done", "v_inv_done", "v_tanh_done",
                                                  "f_exp_done", "o_raw_done", "o_norm_done", "o_inv_done",
                                                  "clip_done", "gated_done", "f_done"))

        block = stack.enter_context(nc.Block())

        @block.sync
        def _(sp):
            def load_ctx(b):
                if not isinstance(b, int) or b > 0:
                    sp.wait_ge(turned, turn(b - 2, "C1")[1] if not isinstance(b, int) or b > 1 else turn(None, "C1")[1])
                sp.dma_start(ctx_rows[:, :, :], ctx[b].rearrange("(t p) c -> p t c", p=P)).then_inc(ctx_in, 16)

            def load_x(b, l):
                if not isinstance(b, int) or b > 0:
                    sp.wait_ge(y_done, T * (b - 1) + l + 1)
                sp.dma_start(x_rows[:, l, :], x[b, l * P:(l + 1) * P, :]).then_inc(x_in[l], 16)

            def store(b, l):
                sp.wait_ge(final_done, T * b + l + 1)
                sp.dma_start(out[b, l * P:(l + 1) * P, :], t_rows[:, l, :]).then_inc(stored[l], 16)

            def body(b, first=False, front=True):
                if front:
                    load_ctx(b + 1)
                for l in range(T):
                    if front:
                        load_x(b + 1, l)
                    if l == 1 and not first:
                        store(b - 1, 2)
                        store(b - 1, 3)
                store(b, 0)
                store(b, 1)

            load_ctx(0)
            for l in range(T):
                load_x(0, l)
            sp.dma_start(w_rows[:, :, :], w.rearrange("(t p) n -> p t n", p=P)).then_inc(w_in, 16)
            sp.dma_start(scale_all[:, :], scale.rearrange("(a n) -> a n", a=1).to_broadcast([P, N])).then_inc(scale_in, 16)
            body(0, first=True)
            with sp.Fori(1, LAST) as b:
                body(b)
            body(LAST, front=False)
            store(LAST, 2)
            store(LAST, 3)
            for l in range(T):
                sp.wait_ge(stored[l], 16 * B)

        @block.gpsimd
        def _(pool):
            def count(value):
                return value if isinstance(value, int) else pool.to_reg(value)

            def layer_norm_x(b, l):
                n = count(T * b + l + 1)
                pool.wait_ge(consts_done, 2)
                pool.wait_ge(x_mv_done, n)
                pool.tensor_scalar(x_ve[:, l:l + 1], x_mv[:, l, 1:2], LN_EPS, 0.0, ALU.add, ALU.add).then_inc(x_ve_done, 1)
                pool.tensor_scalar(x_nm[:, l:l + 1], x_mv[:, l, 0:1], -1.0, 0.0, ALU.mult, ALU.add).then_inc(x_nm_done, 1)
                pool.wait_ge(x_ve_done, n)
                pool.tensor_tensor(x_rstd[:, l:l + 1], x_ve[:, l:l + 1], minus_half[:, 0:1], ALU.pow).then_inc(x_rstd_done, 1)
                pool.wait_ge(consts_done, 2)
                pool.wait_ge(x_nm_done, n)
                pool.wait_ge(x_rstd_done, n)
                pool.tensor_scalar(xn[:, l, :], x_rows[:, l, :], x_nm[:, l:l + 1], x_rstd[:, l:l + 1],
                                   ALU.add, ALU.mult).then_inc(xn_done, 1)

            def layer_norm_y(b, l):
                n = count(T * b + l + 1)
                pool.wait_ge(consts_done, 2)
                pool.wait_ge(y_mv_done, n)
                pool.tensor_scalar(y_ve[:, l:l + 1], y_mv[:, l, 1:2], LN_EPS, 0.0, ALU.add, ALU.add).then_inc(y_ve_done, 1)
                pool.tensor_scalar(y_nm[:, l:l + 1], y_mv[:, l, 0:1], -1.0, 0.0, ALU.mult, ALU.add).then_inc(y_nm_done, 1)
                pool.wait_ge(y_ve_done, n)
                pool.tensor_tensor(y_rstd[:, l:l + 1], y_ve[:, l:l + 1], minus_half[:, 0:1], ALU.pow).then_inc(y_rstd_done, 1)
                pool.wait_ge(consts_done, 2)
                pool.wait_ge(y_nm_done, n)
                pool.wait_ge(y_rstd_done, n)
                pool.tensor_scalar(z_rows[:, l % 2, :], y_rows[:, l, :], y_nm[:, l:l + 1], y_rstd[:, l:l + 1],
                                   ALU.add, ALU.mult).then_inc(z_done, 1)

            def normalize(b, m):
                n = count(T * b + m + 1)
                pool.wait_ge(gates_done, 1)
                pool.wait_ge(inv_done, n)
                pool.tensor_scalar(probs_n[:, m, :], probs[:, m, :], inv_sum[:, m:m + 1], tanh_gates[:, 0:1],
                                   ALU.mult, ALU.mult).then_inc(probs_done, 1)

            def ffn_norm(b, h):
                c, n = slice(2 * h, 2 * h + 2), count(2 * b + h + 1)
                pool.wait_ge(sq_done, T * b + 2 * h + 2)
                pool.tensor_tensor(norm[:, c], sq_sum[:, c], half[:, c], ALU.pow).then_inc(norm_done, 1)
                pool.wait_ge(consts_done, 2)
                pool.wait_ge(norm_done, n)
                pool.tensor_scalar(v_norm[:, c], norm[:, c], NORM_EPS, 0.0, ALU.max, ALU.add).then_inc(v_norm_done, 1)
                pool.tensor_scalar(v_eps[:, c], norm[:, c], NORM_EPS, NORM_EPS, ALU.max, ALU.add).then_inc(v_eps_done, 1)

            def ffn_exp(b, h):
                c, n = slice(2 * h, 2 * h + 2), count(2 * b + h + 1)
                pool.wait_ge(v_inv_done, n)
                pool.wait_ge(v_tanh_done, n)
                pool.tensor_tensor(f_exp[:, c], v_tanh[:, c], v_inv[:, c], ALU.mult).then_inc(f_exp_done, 1)
                pool.wait_ge(f_exp_done, n)
                pool.tensor_tensor(o_raw[:, c], norm[:, c], f_exp[:, c], ALU.mult).then_inc(o_raw_done, 1)
                pool.wait_ge(consts_done, 2)
                pool.wait_ge(o_raw_done, n)
                pool.tensor_scalar(o_norm[:, c], o_raw[:, c], NORM_EPS, 0.0, ALU.max, ALU.add).then_inc(o_norm_done, 1)

            def ffn_factor(b, h):
                c, n = slice(2 * h, 2 * h + 2), count(2 * b + h + 1)
                pool.wait_ge(consts_done, 2)
                pool.wait_ge(o_inv_done, n)
                pool.tensor_scalar(clip[:, c], o_inv[:, c], MAX_NORM, 1.0, ALU.mult, ALU.min).then_inc(clip_done, 1)
                pool.wait_ge(consts_done, 2)
                pool.wait_ge(clip_done, n)
                pool.tensor_scalar(clip[:, c], clip[:, c], tanh_gates[:, 1:2], 1.0, ALU.mult, ALU.mult).then_inc(gated_done, 1)
                pool.wait_ge(gated_done, n)
                pool.tensor_tensor(f_all[:, c], clip[:, c], f_exp[:, c], ALU.mult).then_inc(f_done, 1)

            def body(b, first=False, front=True):
                if not first:
                    ffn_norm(b - 1, 1)
                layer_norm_y(b, 0)
                if not first:
                    ffn_exp(b - 1, 1)
                    ffn_factor(b - 1, 1)
                layer_norm_y(b, 1)
                layer_norm_y(b, 2)
                if front:
                    layer_norm_x(b + 1, 0)
                    layer_norm_x(b + 1, 1)
                layer_norm_y(b, 3)
                if front:
                    for m in range(T):
                        normalize(b + 1, m)
                ffn_norm(b, 0)
                ffn_exp(b, 0)
                ffn_factor(b, 0)
                if front:
                    layer_norm_x(b + 1, 2)
                    layer_norm_x(b + 1, 3)

            pool.memset(ident[:, :], 0.0).then_inc(ident_done, 1)
            pool.memset(half[:, :], 0.5).then_inc(consts_done, 1)
            pool.memset(minus_half[:, :], -0.5).then_inc(consts_done, 1)
            pool.wait_ge(ident_done, 1)
            pool.affine_select(out=ident[:, :], in_=ident[:, :], compare_op=ALU.not_equal, fill=1.0, base=0,
                               pattern=[[-1, P]], channel_multiplier=1).then_inc(ident_done, 1)
            layer_norm_x(0, 0)
            for m in range(T):
                normalize(0, m)
            for l in range(1, T):
                layer_norm_x(0, l)
            body(0, first=True)
            with pool.Fori(1, LAST) as b:
                body(b)
            body(LAST, front=False)
            ffn_norm(LAST, 1)
            ffn_exp(LAST, 1)
            ffn_factor(LAST, 1)

        @block.scalar
        def _(act):
            def hi(b, name, dst):
                bank, n = turn(b, name)
                act.wait_ge(turned, n)
                act.activation(dst, turn_ps[bank][:, :], ACT.Copy).then_inc(hi_done, 1)

            def project_hi(b):
                for i, bias in ((0, b_q), (1, b_k)):
                    act.wait_ge(qk_done, 2 * b + i + 1)
                    act.activation(qk_hi[:, i, :], front_ps[i][:, :], ACT.Identity, bias=bias[:, 0:1]).then_inc(qk_hi_done, 1)

            def exp(b, m):
                act.wait_ge(max_done, T * b + m + 1)
                act.activation(probs[:, m, :], front_ps[m % 2][:, :], ACT.Exp, bias=neg_max[:, m:m + 1],
                               accum_out=exp_sum[:, m:m + 1]).then_inc(exp_done, 1)

            def square(b, l):
                act.wait_ge(t_done, T * b + l + 1)
                if not isinstance(b, int) or b > 0 or l > 0:
                    act.wait_ge(sq_done, T * b + l)
                act.activation(squares[:, :], t_rows[:, l, :], ACT.Square, accum_out=sq_sum[:, l:l + 1]).then_inc(sq_done, 1)

            def tanh_norm(b, h):
                c = slice(2 * h, 2 * h + 2)
                act.wait_ge(v_norm_done, 2 * b + h + 1)
                act.activation(v_tanh[:, c], v_norm[:, c], ACT.Tanh).then_inc(v_tanh_done, 1)

            def body(b, first=False, front=True):
                if not first:
                    square(b - 1, 3)
                hi(b, "X1", xt_hi[:, 1, :])
                if not first:
                    tanh_norm(b - 1, 1)
                if front:
                    hi(b, "C0", ct_hi[:, 0, :])
                    hi(b, "C1", ct_hi[:, 1, :])
                hi(b, "X2", xt_hi[:, 0, :])
                hi(b, "Z0", zt_hi[:, 0, :])
                if front:
                    project_hi(b + 1)
                hi(b, "X3", xt_hi[:, 1, :])
                if front:
                    hi(b, "Z1", zt_hi[:, 1, :])
                    square(b, 0)
                    exp(b + 1, 0)
                    exp(b + 1, 1)
                    square(b, 1)
                    exp(b + 1, 2)
                    exp(b + 1, 3)
                    hi(b, "Z2", zt_hi[:, 0, :])
                    hi(b, "X0", xt_hi[:, 0, :])
                    tanh_norm(b, 0)
                    hi(b, "Z3", zt_hi[:, 1, :])
                    hi(b, "P0", pt_hi[:, 0, :])
                    hi(b, "P1", pt_hi[:, 1, :])
                    square(b, 2)
                    hi(b, "P2", pt_hi[:, 2, :])
                    hi(b, "P3", pt_hi[:, 3, :])
                else:
                    square(b, 0)
                    hi(b, "Z1", zt_hi[:, 1, :])
                    square(b, 1)
                    hi(b, "Z2", zt_hi[:, 0, :])
                    tanh_norm(b, 0)
                    square(b, 2)
                    hi(b, "Z3", zt_hi[:, 1, :])

            act.dma_start(wqk_rows[:, 0:C], wq).then_inc(wqk_in, 16)
            act.dma_start(wqk_rows[:, C:2 * C], wk).then_inc(wqk_in, 16)
            act.dma_start(b_q[:, :], bq.rearrange("(d a) -> d a", a=1)).then_inc(small_in, 16)
            act.dma_start(b_k[:, :], bk.rearrange("(d a) -> d a", a=1)).then_inc(small_in, 16)
            act.dma_start(gates[:, 0:1], g_xattn.rearrange("(a n) -> a n", a=1).to_broadcast([P, 1])).then_inc(small_in, 16)
            act.dma_start(gates[:, 1:2], g_ffn.rearrange("(a n) -> a n", a=1).to_broadcast([P, 1])).then_inc(small_in, 16)
            hi(None, "W", wqk_hi[:, :])
            hi(None, "C0", ct_hi[:, 0, :])
            hi(None, "C1", ct_hi[:, 1, :])
            act.wait_ge(small_in, 64)
            act.activation(tanh_gates[:, :], gates[:, :], ACT.Tanh).then_inc(gates_done, 1)
            project_hi(0)
            for m in range(T):
                exp(0, m)
            hi(None, "X0", xt_hi[:, 0, :])
            for j in range(T):
                hi(None, f"P{j}", pt_hi[:, j, :])
            body(0, first=True)
            with act.Fori(1, LAST) as b:
                body(b)
            body(LAST, front=False)
            square(LAST, 3)
            tanh_norm(LAST, 1)

        @block.vector
        def _(dve):
            def count(value):
                return value if isinstance(value, int) else dve.to_reg(value)

            def lo(b, name, dst, hi_part):
                bank, n = turn(b, name)
                dve.wait_ge(hi_done, n)
                dve.tensor_tensor(dst, turn_ps[bank][:, :], hi_part.bitcast(F32), ALU.subtract).then_inc(lo_done, 1)

            def project_lo(b):
                for i, bias in ((0, b_q), (1, b_k)):
                    dve.wait_ge(qk_hi_done, 2 * b + i + 1)
                    dve.scalar_tensor_tensor(out=qk_lo[:, i, :], in0=front_ps[i][:, :], scalar=bias[:, 0:1],
                                             in1=qk_hi[:, i, :].bitcast(F32), op0=ALU.add, op1=ALU.subtract)\
                       .then_inc(qk_lo_done, 1)

            def stats_x(b, l):
                n = count(T * b + l + 1)
                dve.wait_ge(x_in[l], 16 * (b + 1))
                dve.bn_stats(x_bn[:, l, :], x_rows[:, l, :]).then_inc(x_bn_done, 1)
                dve.wait_ge(small_in, 64)
                dve.wait_ge(x_bn_done, n)
                dve.bn_aggr(x_mv[:, l, :], x_bn[:, l, :]).then_inc(x_mv_done, 1)

            def row_max(b, m):
                dve.wait_ge(energy_done, T * b + m + 1)
                dve.reduce_max(neg_max[:, m:m + 1], front_ps[m % 2][:, :], AX_X, negate=True).then_inc(max_done, 1)

            def row_inverse(b, m):
                dve.wait_ge(exp_done, T * b + m + 1)
                dve.reciprocal(inv_sum[:, m:m + 1], exp_sum[:, m:m + 1]).then_inc(inv_done, 1)

            def add_attention(b, l):
                n = count(T * b + l + 1)
                if not isinstance(b, int) or b > 0:
                    dve.wait_ge(final_done, T * (b - 1) + l + 1)
                dve.wait_ge(pv_done, n)
                dve.tensor_tensor(y_rows[:, l, :], pv_ps[l % 2][:, :], x_rows[:, l, :], ALU.add).then_inc(y_done, 1)
                dve.wait_ge(y_done, n)
                dve.bn_stats(y_bn[:, l, :], y_rows[:, l, :]).then_inc(y_bn_done, 1)
                dve.wait_ge(small_in, 64)
                dve.wait_ge(y_bn_done, n)
                dve.bn_aggr(y_mv[:, l, :], y_bn[:, l, :]).then_inc(y_mv_done, 1)

            def scale_ffn(b, l):
                dve.wait_ge(ffn_done, T * b + l + 1)
                if not isinstance(b, int) or b > 0:
                    dve.wait_ge(stored[l], 16 * b)
                else:
                    dve.wait_ge(scale_in, 16)
                dve.tensor_tensor(t_rows[:, l, :], ffn_ps[l % 2][:, :], scale_all[:, :], ALU.mult).then_inc(t_done, 1)

            def invert_v(b, h):
                c = slice(2 * h, 2 * h + 2)
                dve.wait_ge(v_eps_done, 2 * b + h + 1)
                dve.reciprocal(v_inv[:, c], v_eps[:, c]).then_inc(v_inv_done, 1)

            def invert_o(b, h):
                c = slice(2 * h, 2 * h + 2)
                dve.wait_ge(o_norm_done, 2 * b + h + 1)
                dve.reciprocal(o_inv[:, c], o_norm[:, c]).then_inc(o_inv_done, 1)

            def final(b, l):
                dve.wait_ge(f_done, 2 * b + l // 2 + 1)
                dve.scalar_tensor_tensor(out=t_rows[:, l, :], in0=t_rows[:, l, :], scalar=f_all[:, l:l + 1],
                                         in1=y_rows[:, l, :], op0=ALU.mult, op1=ALU.add).then_inc(final_done, 1)

            def split_w():
                dve.wait_ge(w_in, 16)
                for j in range(T):
                    dve.tensor_copy(w_hi[:, j, :], w_rows[:, j, :]).then_inc(w_hi_done, 1)
                for j in range(T):
                    dve.wait_ge(w_hi_done, j + 1)
                    dve.tensor_tensor(w_lo[:, j, :], w_rows[:, j, :], w_hi[:, j, :].bitcast(F32), ALU.subtract)\
                       .then_inc(w_lo_done, 1)

            def lo_x(b, l):
                lo(b, f"X{l}", xt_lo[:, l % 2, :], xt_hi[:, l % 2, :])

            def lo_z(b, l):
                lo(b, f"Z{l}", zt_lo[:, l % 2, :], zt_hi[:, l % 2, :])

            def lo_c(b, j):
                lo(b, f"C{j}", ct_lo[:, j, :], ct_hi[:, j, :])

            def lo_p(b, j):
                lo(b, f"P{j}", pt_lo[:, j, :], pt_hi[:, j, :])

            def body(b, first=False, front=True):
                if not first:
                    scale_ffn(b - 1, 3)
                add_attention(b, 0)
                if first:
                    split_w()
                else:
                    invert_v(b - 1, 1)
                lo_x(b, 1)
                if not first:
                    invert_o(b - 1, 1)
                add_attention(b, 1)
                if front:
                    lo_c(b, 0)
                    lo_c(b, 1)
                lo_x(b, 2)
                lo_z(b, 0)
                if not first:
                    final(b - 1, 2)
                    final(b - 1, 3)
                add_attention(b, 2)
                if front:
                    project_lo(b + 1)
                lo_x(b, 3)
                if front:
                    stats_x(b + 1, 0)
                    lo_z(b, 1)
                    stats_x(b + 1, 1)
                    scale_ffn(b, 0)
                    add_attention(b, 3)
                    row_max(b + 1, 0)
                    row_max(b + 1, 1)
                    row_inverse(b + 1, 0)
                    row_inverse(b + 1, 1)
                    scale_ffn(b, 1)
                    row_max(b + 1, 2)
                    row_max(b + 1, 3)
                    row_inverse(b + 1, 2)
                    lo_z(b, 2)
                    row_inverse(b + 1, 3)
                    stats_x(b + 1, 2)
                    lo_x(b, 0)
                    scale_ffn(b, 2)
                    invert_v(b, 0)
                    lo_z(b, 3)
                    lo_p(b, 0)
                    invert_o(b, 0)
                    lo_p(b, 1)
                    final(b, 0)
                    lo_p(b, 2)
                    lo_p(b, 3)
                    final(b, 1)
                    stats_x(b + 1, 3)
                else:
                    scale_ffn(b, 0)
                    lo_z(b, 1)
                    add_attention(b, 3)
                    scale_ffn(b, 1)
                    lo_z(b, 2)
                    invert_v(b, 0)
                    scale_ffn(b, 2)
                    lo_z(b, 3)
                    invert_o(b, 0)
                    final(b, 0)
                    final(b, 1)

            lo(None, "W", wqk_lo[:, :], wqk_hi[:, :])
            lo_c(None, 0)
            lo_c(None, 1)
            dve.wait_ge(small_in, 64)
            project_lo(0)
            stats_x(0, 0)
            row_max(0, 0)
            row_max(0, 1)
            row_inverse(0, 0)
            row_max(0, 2)
            row_inverse(0, 1)
            row_max(0, 3)
            row_inverse(0, 2)
            row_inverse(0, 3)
            lo_x(None, 0)
            stats_x(0, 1)
            for j in range(T):
                lo_p(None, j)
            stats_x(0, 2)
            stats_x(0, 3)
            body(0, first=True)
            with dve.Fori(1, LAST) as b:
                body(b)
            body(LAST, front=False)
            scale_ffn(LAST, 3)
            invert_v(LAST, 1)
            invert_o(LAST, 1)
            final(LAST, 2)
            final(LAST, 3)

        @block.tensor
        def _(pe):
            def transposes(b, name, sources):
                bank, n = turn(b, name)
                if not isinstance(n, int) or n > 2:
                    pe.wait_ge(lo_done, n - 2)
                for i, source in enumerate(sources):
                    last = pe.transpose(turn_ps[bank][:, i * P:(i + 1) * P], source, ident[:, :])
                last.then_inc(turned, 1)

            def split_product(dst, lhs_hi, lhs_lo, rhs_hi, rhs_lo, start, stop):
                pe.matmul(dst, lhs_hi, rhs_hi, start=start, stop=False)
                pe.matmul(dst, lhs_lo, rhs_hi, start=False, stop=False)
                return pe.matmul(dst, lhs_hi, rhs_lo, start=False, stop=stop)

            def blocks(rows):
                return [rows[:, j * P:(j + 1) * P] for j in range(T)]

            def turn_x(b, b_of_x, l):
                pe.wait_ge(xn_done, T * b_of_x + l + 1)
                transposes(b, f"X{l}", blocks(xn[:, l, :]))

            def turn_z(b, l):
                pe.wait_ge(z_done, T * b + l + 1)
                transposes(b, f"Z{l}", blocks(z_rows[:, l % 2, :]))

            def turn_ctx(b, b_of_ctx):
                pe.wait_ge(ctx_in, 16 * (b_of_ctx + 1))
                for j in range(CT):
                    transposes(b, f"C{j}", [ctx_rows[:, t, j * P:(j + 1) * P] for t in range(T)])

            def turn_probs(b, b_of_p, j):
                if j == 0:
                    pe.wait_ge(probs_done, T * (b_of_p + 1))
                transposes(b, f"P{j}", [probs_n[:, m, j * P:(j + 1) * P] for m in range(T)])

            def project(b_turn, b):
                pe.wait_ge(lo_done, turn(b_turn, "C1")[1])
                for i in range(2):
                    if not isinstance(b, int) or b > 0:
                        pe.wait_ge(exp_done, T * b - 1 + i)
                    for j in range(CT):
                        c = slice((i * CT + j) * P, (i * CT + j + 1) * P)
                        last = split_product(front_ps[i][:, :], wqk_hi[:, c], wqk_lo[:, c], ct_hi[:, j, :],
                                             ct_lo[:, j, :], j == 0, j == CT - 1)
                    last.then_inc(qk_done, 1)

            def energy(b, m):
                if m < 2:
                    pe.wait_ge(qk_lo_done, 2 * (b + 1))
                else:
                    pe.wait_ge(exp_done, T * b + m - 1)
                c = slice(m * P, (m + 1) * P)
                split_product(front_ps[m % 2][:, :], qk_hi[:, 0, c], qk_lo[:, 0, c], qk_hi[:, 1, :], qk_lo[:, 1, :],
                              True, True).then_inc(energy_done, 1)

            def attend(b, l, b_probs):
                if l == 0:
                    pe.wait_ge(lo_done, turn(b_probs, "X0")[1])
                else:
                    pe.wait_ge(lo_done, turn(b, f"X{l}")[1])
                if not isinstance(b, int) or b > 0 or l >= 2:
                    pe.wait_ge(y_done, T * b + l - 1)
                for j in range(T):
                    if l == 0:
                        pe.wait_ge(lo_done, turn(b_probs, f"P{j}")[1])
                    c = slice(j * P, (j + 1) * P)
                    last = split_product(pv_ps[l % 2][:, :], xt_hi[:, l % 2, c], xt_lo[:, l % 2, c], pt_hi[:, j, :],
                                         pt_lo[:, j, :], j == 0, j == T - 1)
                last.then_inc(pv_done, 1)

            def ffn(b, l, j):
                if j == 0:
                    pe.wait_ge(lo_done, turn(b, f"Z{l}")[1])
                    if not isinstance(b, int) or b > 0 or l >= 2:
                        pe.wait_ge(t_done, T * b + l - 1)
                    else:
                        pe.wait_ge(w_lo_done, T)
                c = slice(j * P, (j + 1) * P)
                last = split_product(ffn_ps[l % 2][:, :], zt_hi[:, l % 2, c], zt_lo[:, l % 2, c], w_hi[:, j, :],
                                     w_lo[:, j, :], j == 0, j == T - 1)
                if j == T - 1:
                    last.then_inc(ffn_done, 1)

            def body(b, first=False, front=True):
                attend(b, 0, None if first else b - 1)
                turn_x(b, b, 1)
                attend(b, 1, None)
                if front:
                    turn_ctx(b, b + 1)
                turn_x(b, b, 2)
                turn_z(b, 0)
                attend(b, 2, None)
                if front:
                    project(b, b + 1)
                turn_x(b, b, 3)
                if front:
                    turn_z(b, 1)
                for j in range(T):
                    ffn(b, 0, j)
                if not front:
                    turn_z(b, 1)
                attend(b, 3, None)
                if front:
                    energy(b + 1, 0)
                    energy(b + 1, 1)
                for j in range(T):
                    ffn(b, 1, j)
                if front:
                    energy(b + 1, 2)
                    energy(b + 1, 3)
                turn_z(b, 2)
                for j in range(T):
                    ffn(b, 2, j)
                if front:
                    turn_x(b, b + 1, 0)
                turn_z(b, 3)
                for j in range(T):
                    if front:
                        turn_probs(b, b + 1, j)
                    ffn(b, 3, j)

            pe.wait_ge(ident_done, 2)
            pe.wait_ge(wqk_in, 32)
            transposes(None, "W", blocks(wqk_rows))
            turn_ctx(None, 0)
            project(None, 0)
            for m in range(T):
                energy(0, m)
            turn_x(None, 0, 0)
            for j in range(T):
                turn_probs(None, 0, j)
            body(0, first=True)
            with pe.Fori(1, LAST) as b:
                body(b)
            body(LAST, front=False)


INS = ["x", "ctx_1024", "g_xattn", "g_ffn", "L0_xattn_Wq", "L0_xattn_bq", "L0_xattn_Wk", "L0_xattn_bk",
       "L0_ffn_weight", "L0_ffn_scale"]


def kernel(**inputs):
    import numpy as np
    import concourse.bacc as bacc
    from concourse.bass_utils import run_bass_kernel_spmd

    nc = bacc.Bacc("TRN2", target_bir_lowering=False, num_devices=1)
    arrays, args = {}, []
    for name in INS:
        a = np.ascontiguousarray(inputs[name])
        if a.ndim == 0:
            a = a.reshape(1)
        arrays[f"in_{name}"] = a
        args.append(nc.dram_tensor(f"in_{name}", a.shape, mybir.dt.from_np(a.dtype), kind="ExternalInput").ap())
    out = nc.dram_tensor("out_0", arrays["in_x"].shape, F32, kind="ExternalOutput").ap()
    gated_block(nc, *args, out)
    r = run_bass_kernel_spmd(nc, [arrays], core_ids=[0])
    return r.results[0]["out_0"]
```

```python
from contextlib import ExitStack

import concourse.bass as bass
from concourse import mybir

F32 = mybir.dt.float32
F32R = mybir.dt.float32r
ALU = mybir.AluOpType
ACT = mybir.ActivationFunctionType
AX_X = mybir.AxisListType.X

LN_EPS = 1e-5
NORM_EPS = 1e-7
MAX_NORM = 0.99
WARM_UP = 10

TURNS_PROLOGUE = ["C0", "C1", "W", "X0", "X1", "P0", "P1", "P2", "P3"]
TURNS_BODY = ["X2", "C0", "C1", "X3", "Z0", "X0", "Z1", "X1", "Z2", "Z3", "P0", "P1", "P2", "P3"]
TURNS_LAST = ["X2", "X3", "Z0", "Z1", "Z2", "Z3"]


def gated_block(nc, x, ctx, g_xattn, g_ffn, wq, bq, wk, bk, w, scale, out):
    P = 128
    B, S, N = x.shape
    C = ctx.shape[2]
    D = wq.shape[0]
    T = S // P
    CT = C // P
    assert (T, CT, D, N, S) == (4, 2, P, T * P, T * P)
    LAST = B - 1

    def turn(b, name):
        if b is None:
            k = TURNS_PROLOGUE.index(name)
            return k % 2, k + 1
        names = TURNS_LAST if isinstance(b, int) and b == LAST else TURNS_BODY
        k = names.index(name)
        return (len(TURNS_PROLOGUE) + k) % 2, len(TURNS_PROLOGUE) + len(TURNS_BODY) * b + k + 1

    with ExitStack() as stack:
        def sbuf(name, shape, dt=F32):
            return stack.enter_context(nc.sbuf_tensor(name, shape, dt))

        def psum(name):
            return stack.enter_context(nc.psum_tensor(name, [P, 512], F32))

        def sem(name):
            return stack.enter_context(nc.semaphore(name))

        x_rows = sbuf("x_rows", [P, T, N])
        ctx_rows = sbuf("ctx_rows", [P, T, C])
        wqk_rows = sbuf("wqk_rows", [P, 2 * C])
        w_rows = sbuf("w_rows", [P, T, N])
        scale_all = sbuf("scale_all", [P, N])
        b_q = sbuf("b_q", [P, 1])
        b_k = sbuf("b_k", [P, 1])
        gates = sbuf("gates", [P, 2])
        tanh_gates = sbuf("tanh_gates", [P, 2])
        warm = sbuf("warm", [P, N], mybir.dt.bfloat16)
        ident = sbuf("ident", [P, P])
        half = sbuf("half", [P, T])
        minus_half = sbuf("minus_half", [P, T])
        wqk_hi, wqk_lo = (sbuf(f"wqk_{s}", [P, 2 * C], F32R) for s in ("hi", "lo"))
        ct_hi, ct_lo = (sbuf(f"ct_{s}", [P, CT, S], F32R) for s in ("hi", "lo"))
        qk_hi, qk_lo = (sbuf(f"qk_{s}", [P, 2, S], F32R) for s in ("hi", "lo"))
        pt_hi, pt_lo = (sbuf(f"pt_{s}", [P, T, S], F32R) for s in ("hi", "lo"))
        xt_hi, xt_lo = (sbuf(f"xt_{s}", [P, 2, N], F32R) for s in ("hi", "lo"))
        zt_hi, zt_lo = (sbuf(f"zt_{s}", [P, 2, N], F32R) for s in ("hi", "lo"))
        w_hi, w_lo = (sbuf(f"w_{s}", [P, T, N], F32R) for s in ("hi", "lo"))
        probs = sbuf("probs", [P, T, S])
        probs_n = sbuf("probs_n", [P, T, S])
        xn = sbuf("xn", [P, T, N])
        y_rows = sbuf("y_rows", [P, T, N])
        z_rows = sbuf("z_rows", [P, 2, N])
        t_rows = sbuf("t_rows", [P, T, N])
        squares = sbuf("squares", [P, N])
        neg_max, exp_sum, inv_sum = (sbuf(n, [P, T]) for n in ("neg_max", "exp_sum", "inv_sum"))
        x_bn, y_bn = (sbuf(n, [P, T, 6]) for n in ("x_bn", "y_bn"))
        x_mv, y_mv = (sbuf(n, [P, T, 2]) for n in ("x_mv", "y_mv"))
        x_ve, x_rstd, x_nm = (sbuf(n, [P, T]) for n in ("x_ve", "x_rstd", "x_nm"))
        y_ve, y_rstd, y_nm = (sbuf(n, [P, T]) for n in ("y_ve", "y_rstd", "y_nm"))
        sq_sum, norm, v_norm, v_eps, v_inv, v_tanh, f_exp, o_raw, o_norm, o_inv, clip, f_all = (
            sbuf(n, [P, T]) for n in ("sq_sum", "norm", "v_norm", "v_eps", "v_inv", "v_tanh", "f_exp",
                                      "o_raw", "o_norm", "o_inv", "clip", "f_all"))

        turn_ps = [psum(f"turn_ps{i}") for i in range(2)]
        front_ps = [psum(f"front_ps{i}") for i in range(2)]
        pv_ps = [psum(f"pv_ps{i}") for i in range(2)]
        ffn_ps = [psum(f"ffn_ps{i}") for i in range(2)]
        prologue_ps = front_ps + ffn_ps

        ctx_in, wqk_in, small_in, w_in, scale_in = (sem(n) for n in ("ctx_in", "wqk_in", "small_in", "w_in", "scale_in"))
        x_in = [sem(f"x_in{l}") for l in range(T)]
        stored = [sem(f"stored{l}") for l in range(T)]
        turned, hi_done, lo_done = sem("turned"), sem("hi_done"), sem("lo_done")
        consts_done, ident_done, gates_done = sem("consts_done"), sem("ident_done"), sem("gates_done")
        warm_done = sem("warm_done")
        w_hi_done, w_lo_done = sem("w_hi_done"), sem("w_lo_done")
        qk_done, qk_hi_done, qk_lo_done = sem("qk_done"), sem("qk_hi_done"), sem("qk_lo_done")
        energy_done, max_done, exp_done, inv_done, probs_done = (
            sem(n) for n in ("energy_done", "max_done", "exp_done", "inv_done", "probs_done"))
        x_bn_done, x_mv_done, x_ve_done, x_rstd_done, x_nm_done, xn_done = (
            sem(n) for n in ("x_bn_done", "x_mv_done", "x_ve_done", "x_rstd_done", "x_nm_done", "xn_done"))
        pv_done, y_done, y_bn_done, y_mv_done, y_ve_done, y_rstd_done, y_nm_done, z_done = (
            sem(n) for n in ("pv_done", "y_done", "y_bn_done", "y_mv_done", "y_ve_done", "y_rstd_done", "y_nm_done",
                             "z_done"))
        ffn_done, t_done, sq_done, final_done = (sem(n) for n in ("ffn_done", "t_done", "sq_done", "final_done"))
        norm_done, v_norm_done, v_eps_done, v_inv_done, v_tanh_done, f_exp_done, o_raw_done, o_norm_done, o_inv_done, \
            clip_done, gated_done, f_done = (sem(n) for n in ("norm_done", "v_norm_done", "v_eps_done", "v_inv_done", "v_tanh_done",
                                                  "f_exp_done", "o_raw_done", "o_norm_done", "o_inv_done",
                                                  "clip_done", "gated_done", "f_done"))

        block = stack.enter_context(nc.Block())

        @block.sync
        def _(sp):
            def load_ctx(b):
                if not isinstance(b, int) or b > 0:
                    sp.wait_ge(turned, turn(b - 2, "C1")[1] if not isinstance(b, int) or b > 1 else turn(None, "C1")[1])
                sp.dma_start(ctx_rows[:, :, :], ctx[b].rearrange("(t p) c -> p t c", p=P)).then_inc(ctx_in, 16)

            def load_x(b, l):
                if not isinstance(b, int) or b > 0:
                    sp.wait_ge(y_done, T * (b - 1) + l + 1)
                sp.dma_start(x_rows[:, l, :], x[b, l * P:(l + 1) * P, :]).then_inc(x_in[l], 16)

            def store(b, l):
                sp.wait_ge(final_done, T * b + l + 1)
                sp.dma_start(out[b, l * P:(l + 1) * P, :], t_rows[:, l, :]).then_inc(stored[l], 16)

            def body(b, first=False, front=True):
                if front:
                    load_ctx(b + 1)
                for l in range(T):
                    if front:
                        load_x(b + 1, l)
                    if l == 0 and not first:
                        store(b - 1, 0)
                        store(b - 1, 1)
                    if l == 1 and not first:
                        store(b - 1, 2)
                        store(b - 1, 3)

            load_ctx(0)
            for l in range(T):
                load_x(0, l)
            sp.dma_start(w_rows[:, :, :], w.rearrange("(t p) n -> p t n", p=P)).then_inc(w_in, 16)
            sp.dma_start(scale_all[:, :], scale.rearrange("(a n) -> a n", a=1).to_broadcast([P, N])).then_inc(scale_in, 16)
            body(0, first=True)
            with sp.Fori(1, LAST) as b:
                body(b)
            body(LAST, front=False)
            for l in range(T):
                store(LAST, l)
            for l in range(T):
                sp.wait_ge(stored[l], 16 * B)

        @block.gpsimd
        def _(pool):
            def count(value):
                return value if isinstance(value, int) else pool.to_reg(value)

            def layer_norm_x(b, l):
                n = count(T * b + l + 1)
                pool.wait_ge(consts_done, 2)
                pool.wait_ge(x_mv_done, n)
                pool.tensor_scalar(x_ve[:, l:l + 1], x_mv[:, l, 1:2], LN_EPS, 0.0, ALU.add, ALU.add).then_inc(x_ve_done, 1)
                pool.tensor_scalar(x_nm[:, l:l + 1], x_mv[:, l, 0:1], -1.0, 0.0, ALU.mult, ALU.add).then_inc(x_nm_done, 1)
                pool.wait_ge(x_ve_done, n)
                pool.tensor_tensor(x_rstd[:, l:l + 1], x_ve[:, l:l + 1], minus_half[:, 0:1], ALU.pow).then_inc(x_rstd_done, 1)
                pool.wait_ge(consts_done, 2)
                pool.wait_ge(x_nm_done, n)
                pool.wait_ge(x_rstd_done, n)
                pool.tensor_scalar(xn[:, l, :], x_rows[:, l, :], x_nm[:, l:l + 1], x_rstd[:, l:l + 1],
                                   ALU.add, ALU.mult).then_inc(xn_done, 1)

            def layer_norm_y(b, l):
                n = count(T * b + l + 1)
                pool.wait_ge(consts_done, 2)
                pool.wait_ge(y_mv_done, n)
                pool.tensor_scalar(y_ve[:, l:l + 1], y_mv[:, l, 1:2], LN_EPS, 0.0, ALU.add, ALU.add).then_inc(y_ve_done, 1)
                pool.tensor_scalar(y_nm[:, l:l + 1], y_mv[:, l, 0:1], -1.0, 0.0, ALU.mult, ALU.add).then_inc(y_nm_done, 1)
                pool.wait_ge(y_ve_done, n)
                pool.tensor_tensor(y_rstd[:, l:l + 1], y_ve[:, l:l + 1], minus_half[:, 0:1], ALU.pow).then_inc(y_rstd_done, 1)
                pool.wait_ge(consts_done, 2)
                pool.wait_ge(y_nm_done, n)
                pool.wait_ge(y_rstd_done, n)
                pool.tensor_scalar(z_rows[:, l % 2, :], y_rows[:, l, :], y_nm[:, l:l + 1], y_rstd[:, l:l + 1],
                                   ALU.add, ALU.mult).then_inc(z_done, 1)

            def normalize(b, m):
                n = count(T * b + m + 1)
                pool.wait_ge(gates_done, 1)
                pool.wait_ge(inv_done, n)
                pool.tensor_scalar(probs_n[:, m, :], probs[:, m, :], inv_sum[:, m:m + 1], tanh_gates[:, 0:1],
                                   ALU.mult, ALU.mult).then_inc(probs_done, 1)

            def ffn_norm(b, h):
                c, n = slice(2 * h, 2 * h + 2), count(2 * b + h + 1)
                pool.wait_ge(sq_done, T * b + 2 * h + 2)
                pool.tensor_tensor(norm[:, c], sq_sum[:, c], half[:, c], ALU.pow).then_inc(norm_done, 1)
                pool.wait_ge(consts_done, 2)
                pool.wait_ge(norm_done, n)
                pool.tensor_scalar(v_norm[:, c], norm[:, c], NORM_EPS, 0.0, ALU.max, ALU.add).then_inc(v_norm_done, 1)
                pool.tensor_scalar(v_eps[:, c], norm[:, c], NORM_EPS, NORM_EPS, ALU.max, ALU.add).then_inc(v_eps_done, 1)

            def ffn_exp(b, h):
                c, n = slice(2 * h, 2 * h + 2), count(2 * b + h + 1)
                pool.wait_ge(v_inv_done, n)
                pool.wait_ge(v_tanh_done, n)
                pool.tensor_tensor(f_exp[:, c], v_tanh[:, c], v_inv[:, c], ALU.mult).then_inc(f_exp_done, 1)
                pool.wait_ge(f_exp_done, n)
                pool.tensor_tensor(o_raw[:, c], norm[:, c], f_exp[:, c], ALU.mult).then_inc(o_raw_done, 1)
                pool.wait_ge(consts_done, 2)
                pool.wait_ge(o_raw_done, n)
                pool.tensor_scalar(o_norm[:, c], o_raw[:, c], NORM_EPS, 0.0, ALU.max, ALU.add).then_inc(o_norm_done, 1)

            def ffn_factor(b, h):
                c, n = slice(2 * h, 2 * h + 2), count(2 * b + h + 1)
                pool.wait_ge(consts_done, 2)
                pool.wait_ge(o_inv_done, n)
                pool.tensor_scalar(clip[:, c], o_inv[:, c], MAX_NORM, 1.0, ALU.mult, ALU.min).then_inc(clip_done, 1)
                pool.wait_ge(consts_done, 2)
                pool.wait_ge(clip_done, n)
                pool.tensor_scalar(clip[:, c], clip[:, c], tanh_gates[:, 1:2], 1.0, ALU.mult, ALU.mult).then_inc(gated_done, 1)
                pool.wait_ge(gated_done, n)
                pool.tensor_tensor(f_all[:, c], clip[:, c], f_exp[:, c], ALU.mult).then_inc(f_done, 1)

            def body(b, first=False, front=True):
                if not first:
                    ffn_norm(b - 1, 1)
                    ffn_exp(b - 1, 1)
                layer_norm_y(b, 0)
                if not first:
                    ffn_factor(b - 1, 1)
                if front:
                    layer_norm_x(b + 1, 0)
                layer_norm_y(b, 1)
                if front:
                    layer_norm_x(b + 1, 1)
                layer_norm_y(b, 2)
                if front:
                    layer_norm_x(b + 1, 2)
                    normalize(b + 1, 0)
                    normalize(b + 1, 1)
                layer_norm_y(b, 3)
                if front:
                    normalize(b + 1, 2)
                    normalize(b + 1, 3)
                    layer_norm_x(b + 1, 3)
                ffn_norm(b, 0)
                ffn_exp(b, 0)
                ffn_factor(b, 0)

            pool.memset(ident[:, :], 0.0).then_inc(ident_done, 1)
            pool.memset(half[:, :], 0.5).then_inc(consts_done, 1)
            pool.memset(minus_half[:, :], -0.5).then_inc(consts_done, 1)
            pool.wait_ge(ident_done, 1)
            pool.affine_select(out=ident[:, :], in_=ident[:, :], compare_op=ALU.not_equal, fill=1.0, base=0,
                               pattern=[[-1, P]], channel_multiplier=1).then_inc(ident_done, 1)
            for l in range(T):
                layer_norm_x(0, l)
            for m in range(T):
                normalize(0, m)
            body(0, first=True)
            with pool.Fori(1, LAST) as b:
                body(b)
            body(LAST, front=False)
            ffn_norm(LAST, 1)
            ffn_exp(LAST, 1)
            ffn_factor(LAST, 1)

        @block.scalar
        def _(act):
            def hi(b, name, dst):
                bank, n = turn(b, name)
                act.wait_ge(turned, n)
                act.activation(dst, turn_ps[bank][:, :], ACT.Copy).then_inc(hi_done, 1)

            def hi_x(b, l):
                hi(b, f"X{l}", xt_hi[:, l % 2, :])

            def hi_z(b, l):
                hi(b, f"Z{l}", zt_hi[:, l % 2, :])

            def hi_p(b, j):
                hi(b, f"P{j}", pt_hi[:, j, :])

            def project_hi(b):
                for i, bias in ((0, b_q), (1, b_k)):
                    act.wait_ge(qk_done, 2 * b + i + 1)
                    act.activation(qk_hi[:, i, :], front_ps[i][:, :], ACT.Identity, bias=bias[:, 0:1]).then_inc(qk_hi_done, 1)

            def exp(b, m, banks=front_ps):
                act.wait_ge(max_done, T * b + m + 1)
                act.activation(probs[:, m, :], banks[m % len(banks)][:, :], ACT.Exp, bias=neg_max[:, m:m + 1],
                               accum_out=exp_sum[:, m:m + 1]).then_inc(exp_done, 1)

            def square(b, l):
                act.wait_ge(t_done, T * b + l + 1)
                if not isinstance(b, int) or b > 0 or l > 0:
                    act.wait_ge(sq_done, T * b + l)
                act.activation(squares[:, :], t_rows[:, l, :], ACT.Square, accum_out=sq_sum[:, l:l + 1]).then_inc(sq_done, 1)

            def tanh_norm(b, h):
                c = slice(2 * h, 2 * h + 2)
                act.wait_ge(v_norm_done, 2 * b + h + 1)
                act.activation(v_tanh[:, c], v_norm[:, c], ACT.Tanh).then_inc(v_tanh_done, 1)

            def body(b, first=False, front=True):
                if not first:
                    square(b - 1, 3)
                    tanh_norm(b - 1, 1)
                hi_x(b, 2)
                if front:
                    hi(b, "C0", ct_hi[:, 0, :])
                    hi(b, "C1", ct_hi[:, 1, :])
                hi_x(b, 3)
                if front:
                    project_hi(b + 1)
                hi_z(b, 0)
                if front:
                    hi_x(b, 0)
                hi_z(b, 1)
                square(b, 0)
                if front:
                    exp(b + 1, 0)
                    exp(b + 1, 1)
                    hi_x(b, 1)
                    exp(b + 1, 2)
                hi_z(b, 2)
                if front:
                    exp(b + 1, 3)
                square(b, 1)
                hi_z(b, 3)
                tanh_norm(b, 0)
                if front:
                    hi_p(b, 0)
                square(b, 2)
                if front:
                    for j in range(1, T):
                        hi_p(b, j)

            act.dma_start(wqk_rows[:, 0:C], wq).then_inc(wqk_in, 16)
            act.dma_start(wqk_rows[:, C:2 * C], wk).then_inc(wqk_in, 16)
            act.preload_act_table(ACT.Exp)
            act.dma_start(b_q[:, :], bq.rearrange("(d a) -> d a", a=1)).then_inc(small_in, 16)
            act.dma_start(b_k[:, :], bk.rearrange("(d a) -> d a", a=1)).then_inc(small_in, 16)
            act.dma_start(gates[:, 0:1], g_xattn.rearrange("(a n) -> a n", a=1).to_broadcast([P, 1])).then_inc(small_in, 16)
            act.dma_start(gates[:, 1:2], g_ffn.rearrange("(a n) -> a n", a=1).to_broadcast([P, 1])).then_inc(small_in, 16)
            hi(None, "C0", ct_hi[:, 0, :])
            hi(None, "C1", ct_hi[:, 1, :])
            hi(None, "W", wqk_hi[:, :])
            act.wait_ge(small_in, 64)
            act.activation(tanh_gates[:, :], gates[:, :], ACT.Tanh).then_inc(gates_done, 1)
            project_hi(0)
            hi_x(None, 0)
            hi_x(None, 1)
            for m in range(T):
                exp(0, m, prologue_ps)
            for j in range(T):
                hi_p(None, j)
            body(0, first=True)
            with act.Fori(1, LAST) as b:
                body(b)
            body(LAST, front=False)
            square(LAST, 3)
            tanh_norm(LAST, 1)

        @block.vector
        def _(dve):
            def count(value):
                return value if isinstance(value, int) else dve.to_reg(value)

            def lo(b, name, dst, hi_part):
                bank, n = turn(b, name)
                dve.wait_ge(hi_done, n)
                dve.tensor_tensor(dst, turn_ps[bank][:, :], hi_part.bitcast(F32), ALU.subtract).then_inc(lo_done, 1)

            def project_lo(b):
                for i, bias in ((0, b_q), (1, b_k)):
                    dve.wait_ge(qk_hi_done, 2 * b + i + 1)
                    dve.scalar_tensor_tensor(out=qk_lo[:, i, :], in0=front_ps[i][:, :], scalar=bias[:, 0:1],
                                             in1=qk_hi[:, i, :].bitcast(F32), op0=ALU.add, op1=ALU.subtract)\
                       .then_inc(qk_lo_done, 1)

            def stats_x(b, l):
                dve.wait_ge(x_in[l], 16 * (b + 1))
                dve.bn_stats(x_bn[:, l, :], x_rows[:, l, :]).then_inc(x_bn_done, 1)

            def moments_x(b, l):
                n = count(T * b + l + 1)
                dve.wait_ge(small_in, 64)
                dve.wait_ge(x_bn_done, n)
                dve.bn_aggr(x_mv[:, l, :], x_bn[:, l, :]).then_inc(x_mv_done, 1)

            def row_max(b, m, banks=front_ps):
                dve.wait_ge(energy_done, T * b + m + 1)
                dve.reduce_max(neg_max[:, m:m + 1], banks[m % len(banks)][:, :], AX_X, negate=True).then_inc(max_done, 1)

            def row_inverse(b, m):
                dve.wait_ge(exp_done, T * b + m + 1)
                dve.reciprocal(inv_sum[:, m:m + 1], exp_sum[:, m:m + 1]).then_inc(inv_done, 1)

            def add_attention(b, l):
                if not isinstance(b, int) or b > 0:
                    dve.wait_ge(final_done, T * (b - 1) + l + 1)
                dve.wait_ge(pv_done, T * b + l + 1)
                dve.tensor_tensor(y_rows[:, l, :], pv_ps[l % 2][:, :], x_rows[:, l, :], ALU.add).then_inc(y_done, 1)

            def stats_y(b, l):
                dve.wait_ge(y_done, T * b + l + 1)
                dve.bn_stats(y_bn[:, l, :], y_rows[:, l, :]).then_inc(y_bn_done, 1)

            def moments_y(b, l):
                n = count(T * b + l + 1)
                dve.wait_ge(small_in, 64)
                dve.wait_ge(y_bn_done, n)
                dve.bn_aggr(y_mv[:, l, :], y_bn[:, l, :]).then_inc(y_mv_done, 1)

            def scale_ffn(b, l):
                dve.wait_ge(ffn_done, T * b + l + 1)
                if not isinstance(b, int) or b > 0:
                    dve.wait_ge(stored[l], 16 * b)
                else:
                    dve.wait_ge(scale_in, 16)
                dve.tensor_tensor(t_rows[:, l, :], ffn_ps[l % 2][:, :], scale_all[:, :], ALU.mult).then_inc(t_done, 1)

            def invert_v(b, h):
                c = slice(2 * h, 2 * h + 2)
                dve.wait_ge(v_eps_done, 2 * b + h + 1)
                dve.reciprocal(v_inv[:, c], v_eps[:, c]).then_inc(v_inv_done, 1)

            def invert_o(b, h):
                c = slice(2 * h, 2 * h + 2)
                dve.wait_ge(o_norm_done, 2 * b + h + 1)
                dve.reciprocal(o_inv[:, c], o_norm[:, c]).then_inc(o_inv_done, 1)

            def final(b, l):
                dve.wait_ge(f_done, 2 * b + l // 2 + 1)
                dve.scalar_tensor_tensor(out=t_rows[:, l, :], in0=t_rows[:, l, :], scalar=f_all[:, l:l + 1],
                                         in1=y_rows[:, l, :], op0=ALU.mult, op1=ALU.add).then_inc(final_done, 1)

            def split_w():
                dve.wait_ge(w_in, 16)
                for j in range(T):
                    dve.tensor_copy(w_hi[:, j, :], w_rows[:, j, :]).then_inc(w_hi_done, 1)
                for j in range(T):
                    dve.wait_ge(w_hi_done, j + 1)
                    dve.tensor_tensor(w_lo[:, j, :], w_rows[:, j, :], w_hi[:, j, :].bitcast(F32), ALU.subtract)\
                       .then_inc(w_lo_done, 1)

            def lo_x(b, l):
                lo(b, f"X{l}", xt_lo[:, l % 2, :], xt_hi[:, l % 2, :])

            def lo_z(b, l):
                lo(b, f"Z{l}", zt_lo[:, l % 2, :], zt_hi[:, l % 2, :])

            def lo_c(b, j):
                lo(b, f"C{j}", ct_lo[:, j, :], ct_hi[:, j, :])

            def lo_p(b, j):
                lo(b, f"P{j}", pt_lo[:, j, :], pt_hi[:, j, :])

            def body(b, first=False, front=True):
                if first:
                    split_w()
                else:
                    scale_ffn(b - 1, 3)
                add_attention(b, 0)
                lo_x(b, 2)
                stats_y(b, 0)
                if not first:
                    invert_v(b - 1, 1)
                if front:
                    lo_c(b, 0)
                moments_y(b, 0)
                if front:
                    lo_c(b, 1)
                    stats_x(b + 1, 0)
                if not first:
                    invert_o(b - 1, 1)
                if front:
                    moments_x(b + 1, 0)
                add_attention(b, 1)
                lo_x(b, 3)
                stats_y(b, 1)
                if front:
                    project_lo(b + 1)
                moments_y(b, 1)
                if front:
                    stats_x(b + 1, 1)
                lo_z(b, 0)
                if front:
                    moments_x(b + 1, 1)
                if not first:
                    final(b - 1, 2)
                    final(b - 1, 3)
                add_attention(b, 2)
                if front:
                    lo_x(b, 0)
                stats_y(b, 2)
                lo_z(b, 1)
                moments_y(b, 2)
                if front:
                    stats_x(b + 1, 2)
                scale_ffn(b, 0)
                if front:
                    moments_x(b + 1, 2)
                    row_max(b + 1, 0)
                    row_max(b + 1, 1)
                    row_inverse(b + 1, 0)
                    row_inverse(b + 1, 1)
                add_attention(b, 3)
                if front:
                    lo_x(b, 1)
                stats_y(b, 3)
                if front:
                    row_max(b + 1, 2)
                moments_y(b, 3)
                if front:
                    row_max(b + 1, 3)
                lo_z(b, 2)
                if front:
                    row_inverse(b + 1, 2)
                    stats_x(b + 1, 3)
                    row_inverse(b + 1, 3)
                    moments_x(b + 1, 3)
                scale_ffn(b, 1)
                lo_z(b, 3)
                scale_ffn(b, 2)
                invert_v(b, 0)
                if front:
                    lo_p(b, 0)
                invert_o(b, 0)
                if front:
                    lo_p(b, 1)
                final(b, 0)
                if front:
                    lo_p(b, 2)
                final(b, 1)
                if front:
                    lo_p(b, 3)

            dve.memset(warm[:, :], 0.0).then_inc(warm_done, 1)
            lo_c(None, 0)
            lo_c(None, 1)
            lo(None, "W", wqk_lo[:, :], wqk_hi[:, :])
            for l in range(T):
                stats_x(0, l)
                if l > 0:
                    moments_x(0, l - 1)
            moments_x(0, T - 1)
            project_lo(0)
            lo_x(None, 0)
            lo_x(None, 1)
            for m in range(T):
                row_max(0, m, prologue_ps)
                if m > 0:
                    row_inverse(0, m - 1)
            row_inverse(0, T - 1)
            for j in range(T):
                lo_p(None, j)
            body(0, first=True)
            with dve.Fori(1, LAST) as b:
                body(b)
            body(LAST, front=False)
            scale_ffn(LAST, 3)
            invert_v(LAST, 1)
            invert_o(LAST, 1)
            final(LAST, 2)
            final(LAST, 3)

        @block.tensor
        def _(pe):
            def transposes(b, name, sources):
                bank, n = turn(b, name)
                if not isinstance(n, int) or n > 2:
                    pe.wait_ge(lo_done, n - 2)
                for i, source in enumerate(sources):
                    last = pe.transpose(turn_ps[bank][:, i * P:(i + 1) * P], source, ident[:, :])
                last.then_inc(turned, 1)

            def split_product(dst, lhs_hi, lhs_lo, rhs_hi, rhs_lo, start, stop):
                pe.matmul(dst, lhs_hi, rhs_hi, start=start, stop=False)
                pe.matmul(dst, lhs_lo, rhs_hi, start=False, stop=False)
                return pe.matmul(dst, lhs_hi, rhs_lo, start=False, stop=stop)

            def blocks(rows):
                return [rows[:, j * P:(j + 1) * P] for j in range(T)]

            def turn_x(b, b_of_x, l):
                pe.wait_ge(xn_done, T * b_of_x + l + 1)
                transposes(b, f"X{l}", blocks(xn[:, l, :]))

            def turn_z(b, l):
                pe.wait_ge(z_done, T * b + l + 1)
                transposes(b, f"Z{l}", blocks(z_rows[:, l % 2, :]))

            def turn_ctx(b, b_of_ctx, j):
                pe.wait_ge(ctx_in, 16 * (b_of_ctx + 1))
                transposes(b, f"C{j}", [ctx_rows[:, t, j * P:(j + 1) * P] for t in range(T)])

            def turn_probs(b, b_of_p, j):
                if j == 0:
                    pe.wait_ge(probs_done, T * (b_of_p + 1))
                transposes(b, f"P{j}", [probs_n[:, m, j * P:(j + 1) * P] for m in range(T)])

            def project(b_turn, b):
                pe.wait_ge(lo_done, turn(b_turn, "C1" if b_turn is not None else "W")[1])
                for i in range(2):
                    if not isinstance(b, int) or b > 0:
                        pe.wait_ge(exp_done, T * b - 1 + i)
                    for j in range(CT):
                        c = slice((i * CT + j) * P, (i * CT + j + 1) * P)
                        last = split_product(front_ps[i][:, :], wqk_hi[:, c], wqk_lo[:, c], ct_hi[:, j, :],
                                             ct_lo[:, j, :], j == 0, j == CT - 1)
                    last.then_inc(qk_done, 1)

            def energy(b, m, banks=front_ps):
                if m < len(banks):
                    pe.wait_ge(qk_lo_done, 2 * (b + 1))
                else:
                    pe.wait_ge(exp_done, T * b + m - 1)
                c = slice(m * P, (m + 1) * P)
                split_product(banks[m % len(banks)][:, :], qk_hi[:, 0, c], qk_lo[:, 0, c], qk_hi[:, 1, :], qk_lo[:, 1, :],
                              True, True).then_inc(energy_done, 1)

            def attend(b, l, j, b_before=None):
                if j == 0:
                    pe.wait_ge(lo_done, turn(b_before if l < 2 else b, f"X{l}")[1])
                    if not isinstance(b, int) or b > 0 or l >= 2:
                        pe.wait_ge(y_done, T * b + l - 1)
                if l == 0:
                    pe.wait_ge(lo_done, turn(b_before, f"P{j}")[1])
                c = slice(j * P, (j + 1) * P)
                last = split_product(pv_ps[l % 2][:, :], xt_hi[:, l % 2, c], xt_lo[:, l % 2, c], pt_hi[:, j, :],
                                     pt_lo[:, j, :], j == 0, j == T - 1)
                if j == T - 1:
                    last.then_inc(pv_done, 1)

            def ffn(b, l, j):
                if j == 0:
                    pe.wait_ge(lo_done, turn(b, f"Z{l}")[1])
                    if not isinstance(b, int) or b > 0 or l >= 2:
                        pe.wait_ge(t_done, T * b + l - 1)
                    else:
                        pe.wait_ge(w_lo_done, T)
                c = slice(j * P, (j + 1) * P)
                last = split_product(ffn_ps[l % 2][:, :], zt_hi[:, l % 2, c], zt_lo[:, l % 2, c], w_hi[:, j, :],
                                     w_lo[:, j, :], j == 0, j == T - 1)
                if j == T - 1:
                    last.then_inc(ffn_done, 1)

            def body(b, first=False, front=True):
                before = None if first else b - 1
                for j in range(T - 1 if first else 0, T):
                    attend(b, 0, j, before)
                turn_x(b, b, 2)
                for j in range(T):
                    attend(b, 1, j, before)
                    if front and j < CT:
                        turn_ctx(b, b + 1, j)
                turn_x(b, b, 3)
                if front:
                    project(b, b + 1)
                    turn_z(b, 0)
                for j in range(T):
                    attend(b, 2, j)
                if front:
                    turn_x(b, b + 1, 0)
                else:
                    turn_z(b, 0)
                    for j in range(T):
                        attend(b, 3, j)
                for j in range(T):
                    ffn(b, 0, j)
                    if j == 0:
                        turn_z(b, 1)
                if front:
                    energy(b + 1, 0)
                    energy(b + 1, 1)
                    for j in range(T):
                        attend(b, 3, j)
                    turn_x(b, b + 1, 1)
                    energy(b + 1, 2)
                    energy(b + 1, 3)
                for j in range(T):
                    ffn(b, 1, j)
                    if j == 0:
                        turn_z(b, 2)
                for j in range(T):
                    ffn(b, 2, j)
                    if j == 0:
                        turn_z(b, 3)
                for j in range(T):
                    if front:
                        turn_probs(b, b + 1, j)
                    ffn(b, 3, j)

            pe.wait_ge(warm_done, 1)
            for i in range(WARM_UP):
                pe.matmul(pv_ps[0][:, :], warm[:, 0:P], warm[:, :], start=i == 0, stop=i == WARM_UP - 1)
            pe.wait_ge(ident_done, 2)
            turn_ctx(None, 0, 0)
            turn_ctx(None, 0, 1)
            pe.wait_ge(wqk_in, 32)
            transposes(None, "W", blocks(wqk_rows))
            project(None, 0)
            turn_x(None, 0, 0)
            turn_x(None, 0, 1)
            for m in range(T):
                energy(0, m, prologue_ps)
            for j in range(T):
                turn_probs(None, 0, j)
                if j > 0:
                    attend(0, 0, j - 1)
            body(0, first=True)
            with pe.Fori(1, LAST) as b:
                body(b)
            body(LAST, front=False)


INS = ["x", "ctx_1024", "g_xattn", "g_ffn", "L0_xattn_Wq", "L0_xattn_bq", "L0_xattn_Wk", "L0_xattn_bk",
       "L0_ffn_weight", "L0_ffn_scale"]


def kernel(**inputs):
    import numpy as np
    import concourse.bacc as bacc
    from concourse.bass_utils import run_bass_kernel_spmd

    nc = bacc.Bacc("TRN2", target_bir_lowering=False, num_devices=1)
    arrays, args = {}, []
    for name in INS:
        a = np.ascontiguousarray(inputs[name])
        if a.ndim == 0:
            a = a.reshape(1)
        arrays[f"in_{name}"] = a
        args.append(nc.dram_tensor(f"in_{name}", a.shape, mybir.dt.from_np(a.dtype), kind="ExternalInput").ap())
    out = nc.dram_tensor("out_0", arrays["in_x"].shape, F32, kind="ExternalOutput").ap()
    gated_block(nc, *args, out)
    r = run_bass_kernel_spmd(nc, [arrays], core_ids=[0])
    return r.results[0]["out_0"]
```

```python
from contextlib import ExitStack

import concourse.bass as bass
from concourse import mybir

F32 = mybir.dt.float32
F32R = mybir.dt.float32r
ALU = mybir.AluOpType
ACT = mybir.ActivationFunctionType
AX_X = mybir.AxisListType.X

LN_EPS = 1e-5
NORM_EPS = 1e-7
MAX_NORM = 0.99
WARM_UP, WARM_SPLIT, WARM_SOFTMAX = 7, 4, 10

TURNS_PROLOGUE = ["C0", "C1", "W", "X0", "X1", "P0", "P1", "P2", "P3"]
TURNS_BODY = ["X2", "C0", "C1", "X3", "Z0", "X0", "Z1", "X1", "Z2", "Z3", "P0", "P1", "P2", "P3"]
TURNS_LAST = ["X2", "X3", "Z0", "Z1", "Z2", "Z3"]


def gated_block(nc, x, ctx, g_xattn, g_ffn, wq, bq, wk, bk, w, scale, out):
    P = 128
    B, S, N = x.shape
    C = ctx.shape[2]
    D = wq.shape[0]
    T = S // P
    CT = C // P
    assert (T, CT, D, N, S) == (4, 2, P, T * P, T * P)
    LAST = B - 1

    def turn(b, name):
        if b is None:
            k = TURNS_PROLOGUE.index(name)
            return 2 if name == "W" else k % 2, k + 1
        names = TURNS_LAST if isinstance(b, int) and b == LAST else TURNS_BODY
        k = names.index(name)
        return (len(TURNS_PROLOGUE) + k) % 2, len(TURNS_PROLOGUE) + len(TURNS_BODY) * b + k + 1

    with ExitStack() as stack:
        def sbuf(name, shape, dt=F32):
            return stack.enter_context(nc.sbuf_tensor(name, shape, dt))

        def psum(name):
            return stack.enter_context(nc.psum_tensor(name, [P, 512], F32))

        def sem(name):
            return stack.enter_context(nc.semaphore(name))

        x_rows = sbuf("x_rows", [P, T, N])
        ctx_rows = sbuf("ctx_rows", [P, T, C])
        wqk_rows = sbuf("wqk_rows", [P, 2 * C])
        w_rows = sbuf("w_rows", [P, T, N])
        scale_all = sbuf("scale_all", [P, N])
        b_q = sbuf("b_q", [P, 1])
        b_k = sbuf("b_k", [P, 1])
        gates = sbuf("gates", [P, 2])
        tanh_gates = sbuf("tanh_gates", [P, 2])
        warm = sbuf("warm", [P, N], mybir.dt.bfloat16)
        ident = sbuf("ident", [P, P])
        half = sbuf("half", [P, T])
        minus_half = sbuf("minus_half", [P, T])
        wqk_hi, wqk_lo = (sbuf(f"wqk_{s}", [P, 2 * C], F32R) for s in ("hi", "lo"))
        ct_hi, ct_lo = (sbuf(f"ct_{s}", [P, CT, S], F32R) for s in ("hi", "lo"))
        qk_hi, qk_lo = (sbuf(f"qk_{s}", [P, 2, S], F32R) for s in ("hi", "lo"))
        pt_hi, pt_lo = (sbuf(f"pt_{s}", [P, T, S], F32R) for s in ("hi", "lo"))
        xt_hi, xt_lo = (sbuf(f"xt_{s}", [P, 2, N], F32R) for s in ("hi", "lo"))
        zt_hi, zt_lo = (sbuf(f"zt_{s}", [P, 2, N], F32R) for s in ("hi", "lo"))
        w_hi, w_lo = (sbuf(f"w_{s}", [P, T, N], F32R) for s in ("hi", "lo"))
        probs = sbuf("probs", [P, T, S])
        probs_n = sbuf("probs_n", [P, T, S])
        xn = sbuf("xn", [P, T, N])
        y_rows = sbuf("y_rows", [P, T, N])
        z_rows = sbuf("z_rows", [P, 2, N])
        t_rows = sbuf("t_rows", [P, T, N])
        squares = sbuf("squares", [P, N])
        neg_max, exp_sum, inv_sum = (sbuf(n, [P, T]) for n in ("neg_max", "exp_sum", "inv_sum"))
        x_bn, y_bn = (sbuf(n, [P, T, 6]) for n in ("x_bn", "y_bn"))
        x_mv, y_mv = (sbuf(n, [P, T, 2]) for n in ("x_mv", "y_mv"))
        x_ve, x_rstd, x_nm = (sbuf(n, [P, T]) for n in ("x_ve", "x_rstd", "x_nm"))
        y_ve, y_rstd, y_nm = (sbuf(n, [P, T]) for n in ("y_ve", "y_rstd", "y_nm"))
        sq_sum, norm, v_norm, v_eps, v_inv, v_tanh, f_exp, o_raw, o_norm, o_inv, clip, f_all = (
            sbuf(n, [P, T]) for n in ("sq_sum", "norm", "v_norm", "v_eps", "v_inv", "v_tanh", "f_exp",
                                      "o_raw", "o_norm", "o_inv", "clip", "f_all"))

        front_ps = [psum(f"front_ps{i}") for i in range(2)]
        pv_ps = [psum(f"pv_ps{i}") for i in range(2)]
        ffn_ps = [psum(f"ffn_ps{i}") for i in range(2)]
        turn_ps = [psum(f"turn_ps{i}") for i in range(2)] + [pv_ps[1]]
        prologue_ps = front_ps + ffn_ps

        ctx_in, wqk_in, small_in, w_in, scale_in = (sem(n) for n in ("ctx_in", "wqk_in", "small_in", "w_in", "scale_in"))
        x_in = [sem(f"x_in{l}") for l in range(T)]
        stored = [sem(f"stored{l}") for l in range(T)]
        turned, hi_done, lo_done = sem("turned"), sem("hi_done"), sem("lo_done")
        consts_done, ident_done, gates_done = sem("consts_done"), sem("ident_done"), sem("gates_done")
        warm_done = sem("warm_done")
        w_hi_done, w_lo_done = sem("w_hi_done"), sem("w_lo_done")
        qk_done, qk_hi_done, qk_lo_done = sem("qk_done"), sem("qk_hi_done"), sem("qk_lo_done")
        energy_done, max_done, exp_done, inv_done, probs_done = (
            sem(n) for n in ("energy_done", "max_done", "exp_done", "inv_done", "probs_done"))
        x_bn_done, x_mv_done, x_ve_done, x_rstd_done, x_nm_done, xn_done = (
            sem(n) for n in ("x_bn_done", "x_mv_done", "x_ve_done", "x_rstd_done", "x_nm_done", "xn_done"))
        pv_done, y_done, y_bn_done, y_mv_done, y_ve_done, y_rstd_done, y_nm_done, z_done = (
            sem(n) for n in ("pv_done", "y_done", "y_bn_done", "y_mv_done", "y_ve_done", "y_rstd_done", "y_nm_done",
                             "z_done"))
        ffn_done, t_done, sq_done, final_done = (sem(n) for n in ("ffn_done", "t_done", "sq_done", "final_done"))
        norm_done, v_norm_done, v_eps_done, v_inv_done, v_tanh_done, f_exp_done, o_raw_done, o_norm_done, o_inv_done, \
            clip_done, gated_done, f_done = (sem(n) for n in ("norm_done", "v_norm_done", "v_eps_done", "v_inv_done", "v_tanh_done",
                                                  "f_exp_done", "o_raw_done", "o_norm_done", "o_inv_done",
                                                  "clip_done", "gated_done", "f_done"))

        tail_step, tail_tanh_done = sem("tail_step"), sem("tail_tanh_done")

        block = stack.enter_context(nc.Block())

        @block.sync
        def _(sp):
            def load_ctx(b):
                if not isinstance(b, int) or b > 0:
                    sp.wait_ge(turned, turn(b - 2, "C1")[1] if not isinstance(b, int) or b > 1 else turn(None, "C1")[1])
                sp.dma_start(ctx_rows[:, :, :], ctx[b].rearrange("(t p) c -> p t c", p=P)).then_inc(ctx_in, 16)

            def load_x(b, l):
                if not isinstance(b, int) or b > 0:
                    sp.wait_ge(y_done, T * (b - 1) + l + 1)
                sp.dma_start(x_rows[:, l, :], x[b, l * P:(l + 1) * P, :]).then_inc(x_in[l], 16)

            def store(b, l):
                sp.wait_ge(final_done, T * b + l + 1)
                sp.dma_start(out[b, l * P:(l + 1) * P, :], t_rows[:, l, :]).then_inc(stored[l], 16)

            def body(b, first=False, front=True):
                if front:
                    load_ctx(b + 1)
                for l in range(T):
                    if front:
                        load_x(b + 1, l)
                    if l == 0 and not first:
                        store(b - 1, 0)
                        store(b - 1, 1)
                    if l == 1 and not first:
                        store(b - 1, 2)
                        store(b - 1, 3)

            load_ctx(0)
            sp.dma_start(b_q[:, :], bq.rearrange("(d a) -> d a", a=1)).then_inc(small_in, 16)
            sp.dma_start(b_k[:, :], bk.rearrange("(d a) -> d a", a=1)).then_inc(small_in, 16)
            sp.dma_start(gates[:, 0:1], g_xattn.rearrange("(a n) -> a n", a=1).to_broadcast([P, 1])).then_inc(small_in, 16)
            sp.dma_start(gates[:, 1:2], g_ffn.rearrange("(a n) -> a n", a=1).to_broadcast([P, 1])).then_inc(small_in, 16)
            for l in range(T):
                load_x(0, l)
            sp.dma_start(w_rows[:, :, :], w.rearrange("(t p) n -> p t n", p=P)).then_inc(w_in, 16)
            sp.dma_start(scale_all[:, :], scale.rearrange("(a n) -> a n", a=1).to_broadcast([P, N])).then_inc(scale_in, 16)
            body(0, first=True)
            with sp.Fori(1, LAST) as b:
                body(b)
            body(LAST, front=False)
            for l in range(T):
                store(LAST, l)
            for l in range(T):
                sp.wait_ge(stored[l], 16 * B)

        @block.gpsimd
        def _(pool):
            def count(value):
                return value if isinstance(value, int) else pool.to_reg(value)

            def layer_norm_x(b, l):
                n = count(T * b + l + 1)
                pool.wait_ge(consts_done, 2)
                pool.wait_ge(x_mv_done, n)
                pool.tensor_scalar(x_ve[:, l:l + 1], x_mv[:, l, 1:2], LN_EPS, 0.0, ALU.add, ALU.add).then_inc(x_ve_done, 1)
                pool.tensor_scalar(x_nm[:, l:l + 1], x_mv[:, l, 0:1], -1.0, 0.0, ALU.mult, ALU.add).then_inc(x_nm_done, 1)
                pool.wait_ge(x_ve_done, n)
                pool.tensor_tensor(x_rstd[:, l:l + 1], x_ve[:, l:l + 1], minus_half[:, 0:1], ALU.pow).then_inc(x_rstd_done, 1)
                pool.wait_ge(consts_done, 2)
                pool.wait_ge(x_nm_done, n)
                pool.wait_ge(x_rstd_done, n)
                pool.tensor_scalar(xn[:, l, :], x_rows[:, l, :], x_nm[:, l:l + 1], x_rstd[:, l:l + 1],
                                   ALU.add, ALU.mult).then_inc(xn_done, 1)

            def layer_norm_y(b, l):
                n = count(T * b + l + 1)
                pool.wait_ge(consts_done, 2)
                pool.wait_ge(y_mv_done, n)
                pool.tensor_scalar(y_ve[:, l:l + 1], y_mv[:, l, 1:2], LN_EPS, 0.0, ALU.add, ALU.add).then_inc(y_ve_done, 1)
                pool.tensor_scalar(y_nm[:, l:l + 1], y_mv[:, l, 0:1], -1.0, 0.0, ALU.mult, ALU.add).then_inc(y_nm_done, 1)
                pool.wait_ge(y_ve_done, n)
                pool.tensor_tensor(y_rstd[:, l:l + 1], y_ve[:, l:l + 1], minus_half[:, 0:1], ALU.pow).then_inc(y_rstd_done, 1)
                pool.wait_ge(consts_done, 2)
                pool.wait_ge(y_nm_done, n)
                pool.wait_ge(y_rstd_done, n)
                pool.tensor_scalar(z_rows[:, l % 2, :], y_rows[:, l, :], y_nm[:, l:l + 1], y_rstd[:, l:l + 1],
                                   ALU.add, ALU.mult).then_inc(z_done, 1)

            def normalize(b, m):
                n = count(T * b + m + 1)
                pool.wait_ge(gates_done, 1)
                pool.wait_ge(inv_done, n)
                pool.tensor_scalar(probs_n[:, m, :], probs[:, m, :], inv_sum[:, m:m + 1], tanh_gates[:, 0:1],
                                   ALU.mult, ALU.mult).then_inc(probs_done, 1)

            def ffn_norm(b, h, c=None):
                c, n = c or slice(2 * h, 2 * h + 2), count(2 * b + h + 1)
                pool.wait_ge(sq_done, T * b + c.stop)
                pool.tensor_tensor(norm[:, c], sq_sum[:, c], half[:, c], ALU.pow).then_inc(norm_done, 1)
                pool.wait_ge(consts_done, 2)
                pool.wait_ge(norm_done, n)
                pool.tensor_scalar(v_norm[:, c], norm[:, c], NORM_EPS, 0.0, ALU.max, ALU.add).then_inc(v_norm_done, 1)
                pool.tensor_scalar(v_eps[:, c], norm[:, c], NORM_EPS, NORM_EPS, ALU.max, ALU.add).then_inc(v_eps_done, 1)

            def ffn_exp(b, h, c=None):
                c, n = c or slice(2 * h, 2 * h + 2), count(2 * b + h + 1)
                pool.wait_ge(v_inv_done, n)
                pool.wait_ge(v_tanh_done, n)
                pool.tensor_tensor(f_exp[:, c], v_tanh[:, c], v_inv[:, c], ALU.mult).then_inc(f_exp_done, 1)
                pool.wait_ge(f_exp_done, n)
                pool.tensor_tensor(o_raw[:, c], norm[:, c], f_exp[:, c], ALU.mult).then_inc(o_raw_done, 1)
                pool.wait_ge(consts_done, 2)
                pool.wait_ge(o_raw_done, n)
                pool.tensor_scalar(o_norm[:, c], o_raw[:, c], NORM_EPS, 0.0, ALU.max, ALU.add).then_inc(o_norm_done, 1)

            def ffn_factor(b, h, c=None):
                c, n = c or slice(2 * h, 2 * h + 2), count(2 * b + h + 1)
                pool.wait_ge(consts_done, 2)
                pool.wait_ge(o_inv_done, n)
                pool.tensor_scalar(clip[:, c], o_inv[:, c], MAX_NORM, 1.0, ALU.mult, ALU.min).then_inc(clip_done, 1)
                pool.wait_ge(consts_done, 2)
                pool.wait_ge(clip_done, n)
                pool.tensor_scalar(clip[:, c], clip[:, c], tanh_gates[:, 1:2], 1.0, ALU.mult, ALU.mult).then_inc(gated_done, 1)
                pool.wait_ge(gated_done, n)
                pool.tensor_tensor(f_all[:, c], clip[:, c], f_exp[:, c], ALU.mult).then_inc(f_done, 1)

            def body(b, first=False, front=True):
                if not first:
                    ffn_norm(b - 1, 1)
                    ffn_exp(b - 1, 1)
                layer_norm_y(b, 0)
                if not first:
                    ffn_factor(b - 1, 1)
                if front:
                    layer_norm_x(b + 1, 0)
                layer_norm_y(b, 1)
                if front:
                    layer_norm_x(b + 1, 1)
                layer_norm_y(b, 2)
                if front:
                    layer_norm_x(b + 1, 2)
                    normalize(b + 1, 0)
                    normalize(b + 1, 1)
                layer_norm_y(b, 3)
                if front:
                    normalize(b + 1, 2)
                    normalize(b + 1, 3)
                    layer_norm_x(b + 1, 3)
                ffn_norm(b, 0)
                ffn_exp(b, 0)
                ffn_factor(b, 0)

            pool.memset(ident[:, :], 0.0).then_inc(ident_done, 1)
            pool.memset(half[:, :], 0.5).then_inc(consts_done, 1)
            pool.memset(minus_half[:, :], -0.5).then_inc(consts_done, 1)
            pool.wait_ge(ident_done, 1)
            pool.affine_select(out=ident[:, :], in_=ident[:, :], compare_op=ALU.not_equal, fill=1.0, base=0,
                               pattern=[[-1, P]], channel_multiplier=1).then_inc(ident_done, 1)
            layer_norm_x(0, 0)
            layer_norm_x(0, 1)
            layer_norm_x(0, 2)
            layer_norm_x(0, 3)
            body(0, first=True)
            with pool.Fori(1, LAST) as b:
                body(b)
            body(LAST, front=False)
            ffn_norm(LAST, 1, slice(2, 3))
            ffn_exp(LAST, 1, slice(2, 3))
            pool.wait_ge(sq_done, T * B)
            pool.tensor_tensor(norm[:, 3:4], sq_sum[:, 3:4], half[:, 3:4], ALU.pow).then_inc(norm_done, 1)
            ffn_factor(LAST, 1, slice(2, 3))

        @block.scalar
        def _(act):
            def hi(b, name, dst):
                bank, n = turn(b, name)
                act.wait_ge(turned, n)
                act.activation(dst, turn_ps[bank][:, :], ACT.Copy).then_inc(hi_done, 1)

            def hi_x(b, l):
                hi(b, f"X{l}", xt_hi[:, l % 2, :])

            def hi_z(b, l):
                hi(b, f"Z{l}", zt_hi[:, l % 2, :])

            def hi_p(b, j):
                hi(b, f"P{j}", pt_hi[:, j, :])

            def project_hi(b):
                for i, bias in ((0, b_q), (1, b_k)):
                    act.wait_ge(qk_done, 2 * b + i + 1)
                    act.activation(qk_hi[:, i, :], front_ps[i][:, :], ACT.Identity, bias=bias[:, 0:1]).then_inc(qk_hi_done, 1)

            def exp(b, m, banks=front_ps):
                act.wait_ge(max_done, T * b + m + 1)
                act.activation(probs[:, m, :], banks[m % len(banks)][:, :], ACT.Exp, bias=neg_max[:, m:m + 1],
                               accum_out=exp_sum[:, m:m + 1]).then_inc(exp_done, 1)

            def square(b, l):
                act.wait_ge(t_done, T * b + l + 1)
                if not isinstance(b, int) or b > 0 or l > 0:
                    act.wait_ge(sq_done, T * b + l)
                act.activation(squares[:, :], t_rows[:, l, :], ACT.Square, accum_out=sq_sum[:, l:l + 1]).then_inc(sq_done, 1)

            def tanh_norm(b, h, c=None):
                c = c or slice(2 * h, 2 * h + 2)
                act.wait_ge(v_norm_done, 2 * b + h + 1)
                act.activation(v_tanh[:, c], v_norm[:, c], ACT.Tanh).then_inc(v_tanh_done, 1)

            def body(b, first=False, front=True):
                hi_x(b, 2)
                if not first:
                    square(b - 1, 3)
                if front:
                    hi(b, "C0", ct_hi[:, 0, :])
                    hi(b, "C1", ct_hi[:, 1, :])
                if not first:
                    tanh_norm(b - 1, 1)
                hi_x(b, 3)
                if front:
                    project_hi(b + 1)
                hi_z(b, 0)
                if front:
                    hi_x(b, 0)
                hi_z(b, 1)
                square(b, 0)
                if front:
                    exp(b + 1, 0)
                    exp(b + 1, 1)
                    hi_x(b, 1)
                hi_z(b, 2)
                if front:
                    exp(b + 1, 2)
                    exp(b + 1, 3)
                if not front:
                    square(b, 1)
                hi_z(b, 3)
                if front:
                    square(b, 1)
                    hi_p(b, 0)
                    square(b, 2)
                    hi_p(b, 1)
                    tanh_norm(b, 0)
                    hi_p(b, 2)
                    hi_p(b, 3)
                else:
                    tanh_norm(b, 0)
                    square(b, 2)

            act.dma_start(wqk_rows[:, 0:C], wq).then_inc(wqk_in, 16)
            act.dma_start(wqk_rows[:, C:2 * C], wk).then_inc(wqk_in, 16)
            act.preload_act_table(ACT.Exp)
            hi(None, "C0", ct_hi[:, 0, :])
            hi(None, "C1", ct_hi[:, 1, :])
            hi(None, "W", wqk_hi[:, :])
            act.wait_ge(small_in, 64)
            project_hi(0)
            act.activation(tanh_gates[:, :], gates[:, :], ACT.Tanh).then_inc(gates_done, 1)
            hi_x(None, 0)
            for m in range(T):
                exp(0, m, prologue_ps)
            hi_x(None, 1)
            for j in range(T):
                act.wait_ge(w_in, 16)
                act.activation(w_hi[:, j, :], w_rows[:, j, :], ACT.Copy).then_inc(w_hi_done, 1)
            for j in range(T):
                hi_p(None, j)
            body(0, first=True)
            with act.Fori(1, LAST) as b:
                body(b)
            body(LAST, front=False)
            tanh_norm(LAST, 1, slice(2, 3))
            square(LAST, 3)
            act.wait_ge(tail_step, 1)
            act.activation(v_tanh[:, 3:4], v_norm[:, 3:4], ACT.Tanh).then_inc(tail_tanh_done, 1)

        @block.vector
        def _(dve):
            def count(value):
                return value if isinstance(value, int) else dve.to_reg(value)

            def lo(b, name, dst, hi_part):
                bank, n = turn(b, name)
                dve.wait_ge(hi_done, n)
                dve.tensor_tensor(dst, turn_ps[bank][:, :], hi_part.bitcast(F32), ALU.subtract).then_inc(lo_done, 1)

            def project_lo(b):
                for i, bias in ((0, b_q), (1, b_k)):
                    dve.wait_ge(qk_hi_done, 2 * b + i + 1)
                    dve.scalar_tensor_tensor(out=qk_lo[:, i, :], in0=front_ps[i][:, :], scalar=bias[:, 0:1],
                                             in1=qk_hi[:, i, :].bitcast(F32), op0=ALU.add, op1=ALU.subtract)\
                       .then_inc(qk_lo_done, 1)

            def stats_x(b, l):
                dve.wait_ge(x_in[l], 16 * (b + 1))
                dve.bn_stats(x_bn[:, l, :], x_rows[:, l, :]).then_inc(x_bn_done, 1)

            def moments_x(b, l):
                n = count(T * b + l + 1)
                dve.wait_ge(small_in, 64)
                dve.wait_ge(x_bn_done, n)
                dve.bn_aggr(x_mv[:, l, :], x_bn[:, l, :]).then_inc(x_mv_done, 1)

            def row_max(b, m, banks=front_ps):
                dve.wait_ge(energy_done, T * b + m + 1)
                dve.reduce_max(neg_max[:, m:m + 1], banks[m % len(banks)][:, :], AX_X, negate=True).then_inc(max_done, 1)

            def row_inverse(b, m):
                dve.wait_ge(exp_done, T * b + m + 1)
                dve.reciprocal(inv_sum[:, m:m + 1], exp_sum[:, m:m + 1]).then_inc(inv_done, 1)

            def normalize_first(m):
                dve.wait_ge(gates_done, 1)
                dve.wait_ge(inv_done, m + 1)
                dve.tensor_scalar(probs_n[:, m, :], probs[:, m, :], inv_sum[:, m:m + 1], tanh_gates[:, 0:1],
                                  ALU.mult, ALU.mult).then_inc(probs_done, 1)

            def add_attention(b, l):
                if not isinstance(b, int) or b > 0:
                    dve.wait_ge(final_done, T * (b - 1) + l + 1)
                dve.wait_ge(pv_done, T * b + l + 1)
                dve.tensor_tensor(y_rows[:, l, :], pv_ps[l % 2][:, :], x_rows[:, l, :], ALU.add).then_inc(y_done, 1)

            def stats_y(b, l):
                dve.wait_ge(y_done, T * b + l + 1)
                dve.bn_stats(y_bn[:, l, :], y_rows[:, l, :]).then_inc(y_bn_done, 1)

            def moments_y(b, l):
                n = count(T * b + l + 1)
                dve.wait_ge(small_in, 64)
                dve.wait_ge(y_bn_done, n)
                dve.bn_aggr(y_mv[:, l, :], y_bn[:, l, :]).then_inc(y_mv_done, 1)

            def scale_ffn(b, l):
                dve.wait_ge(ffn_done, T * b + l + 1)
                if not isinstance(b, int) or b > 0:
                    dve.wait_ge(stored[l], 16 * b)
                else:
                    dve.wait_ge(scale_in, 16)
                dve.tensor_tensor(t_rows[:, l, :], ffn_ps[l % 2][:, :], scale_all[:, :], ALU.mult).then_inc(t_done, 1)

            def invert_v(b, h, c=None):
                c = c or slice(2 * h, 2 * h + 2)
                dve.wait_ge(v_eps_done, 2 * b + h + 1)
                dve.reciprocal(v_inv[:, c], v_eps[:, c]).then_inc(v_inv_done, 1)

            def invert_o(b, h, c=None):
                c = c or slice(2 * h, 2 * h + 2)
                dve.wait_ge(o_norm_done, 2 * b + h + 1)
                dve.reciprocal(o_inv[:, c], o_norm[:, c]).then_inc(o_inv_done, 1)

            def final(b, l):
                dve.wait_ge(f_done, 2 * b + l // 2 + 1)
                dve.scalar_tensor_tensor(out=t_rows[:, l, :], in0=t_rows[:, l, :], scalar=f_all[:, l:l + 1],
                                         in1=y_rows[:, l, :], op0=ALU.mult, op1=ALU.add).then_inc(final_done, 1)

            def last_tiles_final():
                c = slice(T - 1, T)
                dve.wait_ge(norm_done, 2 * B + 1)
                dve.tensor_scalar(v_norm[:, c], norm[:, c], NORM_EPS, 0.0, ALU.max, ALU.add).then_inc(tail_step, 1)
                dve.tensor_scalar(v_eps[:, c], norm[:, c], NORM_EPS, NORM_EPS, ALU.max, ALU.add).then_inc(tail_step, 1)
                dve.wait_ge(tail_step, 2)
                dve.reciprocal(v_inv[:, c], v_eps[:, c]).then_inc(tail_step, 1)
                dve.wait_ge(tail_step, 3)
                dve.wait_ge(tail_tanh_done, 1)
                dve.tensor_tensor(f_exp[:, c], v_tanh[:, c], v_inv[:, c], ALU.mult).then_inc(tail_step, 1)
                dve.wait_ge(tail_step, 4)
                dve.tensor_scalar(o_norm[:, c], norm[:, c], f_exp[:, c], NORM_EPS, ALU.mult, ALU.max).then_inc(tail_step, 1)
                final(LAST, 2)
                dve.wait_ge(tail_step, 5)
                dve.reciprocal(o_inv[:, c], o_norm[:, c]).then_inc(tail_step, 1)
                dve.wait_ge(tail_step, 6)
                dve.tensor_scalar(clip[:, c], o_inv[:, c], MAX_NORM, 1.0, ALU.mult, ALU.min).then_inc(tail_step, 1)
                dve.wait_ge(tail_step, 7)
                dve.tensor_scalar(f_all[:, c], clip[:, c], f_exp[:, c], tanh_gates[:, 1:2], ALU.mult, ALU.mult)\
                   .then_inc(tail_step, 1)
                dve.wait_ge(tail_step, 8)
                dve.scalar_tensor_tensor(out=t_rows[:, T - 1, :], in0=t_rows[:, T - 1, :], scalar=f_all[:, c],
                                         in1=y_rows[:, T - 1, :], op0=ALU.mult, op1=ALU.add).then_inc(final_done, 1)

            def w_lo_part(j):
                dve.wait_ge(w_hi_done, j + 1)
                dve.tensor_tensor(w_lo[:, j, :], w_rows[:, j, :], w_hi[:, j, :].bitcast(F32), ALU.subtract)\
                   .then_inc(w_lo_done, 1)

            def lo_x(b, l):
                lo(b, f"X{l}", xt_lo[:, l % 2, :], xt_hi[:, l % 2, :])

            def lo_z(b, l):
                lo(b, f"Z{l}", zt_lo[:, l % 2, :], zt_hi[:, l % 2, :])

            def lo_c(b, j):
                lo(b, f"C{j}", ct_lo[:, j, :], ct_hi[:, j, :])

            def lo_p(b, j):
                lo(b, f"P{j}", pt_lo[:, j, :], pt_hi[:, j, :])

            def body(b, first=False, front=True):
                if not first:
                    scale_ffn(b - 1, 3)
                add_attention(b, 0)
                lo_x(b, 2)
                stats_y(b, 0)
                if front:
                    lo_c(b, 0)
                if not first:
                    invert_v(b - 1, 1)
                moments_y(b, 0)
                if front:
                    lo_c(b, 1)
                    stats_x(b + 1, 0)
                if not first:
                    invert_o(b - 1, 1)
                if front:
                    moments_x(b + 1, 0)
                add_attention(b, 1)
                lo_x(b, 3)
                stats_y(b, 1)
                if front:
                    project_lo(b + 1)
                moments_y(b, 1)
                if front:
                    stats_x(b + 1, 1)
                lo_z(b, 0)
                if front:
                    moments_x(b + 1, 1)
                if not first:
                    final(b - 1, 2)
                    final(b - 1, 3)
                add_attention(b, 2)
                if front:
                    lo_x(b, 0)
                stats_y(b, 2)
                if front:
                    lo_z(b, 1)
                moments_y(b, 2)
                if not front:
                    lo_z(b, 1)
                if front:
                    stats_x(b + 1, 2)
                scale_ffn(b, 0)
                if front:
                    moments_x(b + 1, 2)
                    row_max(b + 1, 0)
                    row_max(b + 1, 1)
                    row_inverse(b + 1, 0)
                add_attention(b, 3)
                if front:
                    row_inverse(b + 1, 1)
                stats_y(b, 3)
                if front:
                    lo_x(b, 1)
                moments_y(b, 3)
                if front:
                    row_max(b + 1, 2)
                lo_z(b, 2)
                if front:
                    row_max(b + 1, 3)
                    row_inverse(b + 1, 2)
                    stats_x(b + 1, 3)
                    row_inverse(b + 1, 3)
                    moments_x(b + 1, 3)
                scale_ffn(b, 1)
                lo_z(b, 3)
                if not front:
                    invert_v(b, 0)
                scale_ffn(b, 2)
                if front:
                    lo_p(b, 0)
                    lo_p(b, 1)
                    invert_v(b, 0)
                    lo_p(b, 2)
                invert_o(b, 0)
                if front:
                    lo_p(b, 3)
                    final(b, 0)
                    final(b, 1)

            dve.memset(warm[:, :], 0.0).then_inc(warm_done, 1)
            lo_c(None, 0)
            lo_c(None, 1)
            lo(None, "W", wqk_lo[:, :], wqk_hi[:, :])
            for l in range(3):
                stats_x(0, l)
                moments_x(0, l)
            project_lo(0)
            lo_x(None, 0)
            row_max(0, 0, prologue_ps)
            row_max(0, 1, prologue_ps)
            row_inverse(0, 0)
            row_max(0, 2, prologue_ps)
            row_inverse(0, 1)
            row_max(0, 3, prologue_ps)
            normalize_first(0)
            normalize_first(1)
            row_inverse(0, 2)
            normalize_first(2)
            row_inverse(0, 3)
            normalize_first(3)
            lo_x(None, 1)
            w_lo_part(0)
            lo_p(None, 0)
            lo_p(None, 1)
            stats_x(0, 3)
            moments_x(0, 3)
            lo_p(None, 2)
            w_lo_part(1)
            lo_p(None, 3)
            w_lo_part(2)
            w_lo_part(3)
            body(0, first=True)
            with dve.Fori(1, LAST) as b:
                body(b)
            body(LAST, front=False)
            final(LAST, 0)
            invert_v(LAST, 1, slice(2, 3))
            scale_ffn(LAST, 3)
            final(LAST, 1)
            invert_o(LAST, 1, slice(2, 3))
            last_tiles_final()

        @block.tensor
        def _(pe):
            def transposes(b, name, sources):
                bank, n = turn(b, name)
                if not isinstance(n, int) or n > 2 and name != "W":
                    pe.wait_ge(lo_done, n - 2)
                for i, source in enumerate(sources):
                    last = pe.transpose(turn_ps[bank][:, i * P:(i + 1) * P], source, ident[:, :])
                last.then_inc(turned, 1)

            def split_product(dst, lhs_hi, lhs_lo, rhs_hi, rhs_lo, start, stop):
                pe.matmul(dst, lhs_hi, rhs_hi, start=start, stop=False)
                pe.matmul(dst, lhs_lo, rhs_hi, start=False, stop=False)
                return pe.matmul(dst, lhs_hi, rhs_lo, start=False, stop=stop)

            def keep_busy(n):
                for i in range(n):
                    pe.matmul(pv_ps[0][:, :], warm[:, 0:P], warm[:, :], start=i == 0, stop=i == n - 1)

            def blocks(rows):
                return [rows[:, j * P:(j + 1) * P] for j in range(T)]

            def turn_x(b, b_of_x, l):
                pe.wait_ge(xn_done, T * b_of_x + l + 1)
                transposes(b, f"X{l}", blocks(xn[:, l, :]))

            def turn_z(b, l):
                pe.wait_ge(z_done, T * b + l + 1)
                transposes(b, f"Z{l}", blocks(z_rows[:, l % 2, :]))

            def turn_ctx(b, b_of_ctx, j):
                pe.wait_ge(ctx_in, 16 * (b_of_ctx + 1))
                transposes(b, f"C{j}", [ctx_rows[:, t, j * P:(j + 1) * P] for t in range(T)])

            def turn_probs(b, b_of_p, j):
                if j == 0:
                    pe.wait_ge(probs_done, T * (b_of_p + 1))
                transposes(b, f"P{j}", [probs_n[:, m, j * P:(j + 1) * P] for m in range(T)])

            def project(b_turn, b):
                pe.wait_ge(lo_done, turn(b_turn, "C1" if b_turn is not None else "W")[1])
                for i in range(2):
                    if not isinstance(b, int) or b > 0:
                        pe.wait_ge(exp_done, T * b - 1 + i)
                    for j in range(CT):
                        c = slice((i * CT + j) * P, (i * CT + j + 1) * P)
                        last = split_product(front_ps[i][:, :], wqk_hi[:, c], wqk_lo[:, c], ct_hi[:, j, :],
                                             ct_lo[:, j, :], j == 0, j == CT - 1)
                    last.then_inc(qk_done, 1)

            def energy(b, m, banks=front_ps):
                if m < len(banks):
                    pe.wait_ge(qk_lo_done, 2 * (b + 1))
                else:
                    pe.wait_ge(exp_done, T * b + m - 1)
                c = slice(m * P, (m + 1) * P)
                split_product(banks[m % len(banks)][:, :], qk_hi[:, 0, c], qk_lo[:, 0, c], qk_hi[:, 1, :], qk_lo[:, 1, :],
                              True, True).then_inc(energy_done, 1)

            def attend(b, l, j, b_before=None):
                if j == 0:
                    pe.wait_ge(lo_done, turn(b_before if l < 2 else b, f"X{l}")[1])
                    if not isinstance(b, int) or b > 0 or l >= 2:
                        pe.wait_ge(y_done, T * b + l - 1)
                if l == 0:
                    pe.wait_ge(lo_done, turn(b_before, f"P{j}")[1])
                c = slice(j * P, (j + 1) * P)
                last = split_product(pv_ps[l % 2][:, :], xt_hi[:, l % 2, c], xt_lo[:, l % 2, c], pt_hi[:, j, :],
                                     pt_lo[:, j, :], j == 0, j == T - 1)
                if j == T - 1:
                    last.then_inc(pv_done, 1)

            def ffn(b, l, j):
                if j == 0:
                    pe.wait_ge(lo_done, turn(b, f"Z{l}")[1])
                    if not isinstance(b, int) or b > 0 or l >= 2:
                        pe.wait_ge(t_done, T * b + l - 1)
                    else:
                        pe.wait_ge(w_lo_done, T)
                c = slice(j * P, (j + 1) * P)
                last = split_product(ffn_ps[l % 2][:, :], zt_hi[:, l % 2, c], zt_lo[:, l % 2, c], w_hi[:, j, :],
                                     w_lo[:, j, :], j == 0, j == T - 1)
                if j == T - 1:
                    last.then_inc(ffn_done, 1)

            def body(b, first=False, front=True):
                before = None if first else b - 1
                for j in range(T - 1 if first else 0, T):
                    attend(b, 0, j, before)
                turn_x(b, b, 2)
                for j in range(T):
                    attend(b, 1, j, before)
                    if front and j < CT:
                        turn_ctx(b, b + 1, j)
                turn_x(b, b, 3)
                if front:
                    project(b, b + 1)
                    turn_z(b, 0)
                for j in range(T):
                    attend(b, 2, j)
                if front:
                    turn_x(b, b + 1, 0)
                else:
                    turn_z(b, 0)
                    for j in range(T):
                        attend(b, 3, j)
                for j in range(T):
                    ffn(b, 0, j)
                    if j == 0:
                        turn_z(b, 1)
                if front:
                    energy(b + 1, 0)
                    energy(b + 1, 1)
                    for j in range(T):
                        attend(b, 3, j)
                    turn_x(b, b + 1, 1)
                    energy(b + 1, 2)
                    energy(b + 1, 3)
                for j in range(T):
                    ffn(b, 1, j)
                    if j == 0:
                        turn_z(b, 2)
                for j in range(T):
                    ffn(b, 2, j)
                    if j == (0 if front else 1):
                        turn_z(b, 3)
                for j in range(T):
                    if front:
                        turn_probs(b, b + 1, j)
                    ffn(b, 3, j)

            pe.wait_ge(warm_done, 1)
            keep_busy(WARM_UP)
            pe.wait_ge(ident_done, 2)
            turn_ctx(None, 0, 0)
            turn_ctx(None, 0, 1)
            pe.wait_ge(wqk_in, 32)
            transposes(None, "W", blocks(wqk_rows))
            keep_busy(WARM_SPLIT)
            project(None, 0)
            turn_x(None, 0, 0)
            for m in range(T):
                energy(0, m, prologue_ps)
            turn_x(None, 0, 1)
            keep_busy(WARM_SOFTMAX)
            turn_probs(None, 0, 0)
            turn_probs(None, 0, 1)
            keep_busy(WARM_SPLIT)
            turn_probs(None, 0, 2)
            attend(0, 0, 0)
            turn_probs(None, 0, 3)
            attend(0, 0, 1)
            attend(0, 0, 2)
            body(0, first=True)
            with pe.Fori(1, LAST) as b:
                body(b)
            body(LAST, front=False)


INS = ["x", "ctx_1024", "g_xattn", "g_ffn", "L0_xattn_Wq", "L0_xattn_bq", "L0_xattn_Wk", "L0_xattn_bk",
       "L0_ffn_weight", "L0_ffn_scale"]


def kernel(**inputs):
    import numpy as np
    import concourse.bacc as bacc
    from concourse.bass_utils import run_bass_kernel_spmd

    nc = bacc.Bacc("TRN2", target_bir_lowering=False, num_devices=1)
    arrays, args = {}, []
    for name in INS:
        a = np.ascontiguousarray(inputs[name])
        if a.ndim == 0:
            a = a.reshape(1)
        arrays[f"in_{name}"] = a
        args.append(nc.dram_tensor(f"in_{name}", a.shape, mybir.dt.from_np(a.dtype), kind="ExternalInput").ap())
    out = nc.dram_tensor("out_0", arrays["in_x"].shape, F32, kind="ExternalOutput").ap()
    gated_block(nc, *args, out)
    r = run_bass_kernel_spmd(nc, [arrays], core_ids=[0])
    return r.results[0]["out_0"]
```
